# Optimizing a Trainium2 kernel written in Bass

```python
import numpy as np
import jax
import jax.numpy as jnp

def _softmax(x, axis=-1):
    return jax.nn.softmax(x, axis=axis)

def _gelu(x):
    return jax.nn.gelu(x, approximate=True)

def _silu(x):
    return jax.nn.silu(x)

def _sigmoid(x):
    return jax.nn.sigmoid(x)

def _layernorm(x, axis=-1, eps=1e-05):
    m = jnp.mean(x, axis=axis, keepdims=True)
    v = jnp.var(x, axis=axis, keepdims=True)
    return (x - m) / jnp.sqrt(v + eps)

def _scatter_add(tgt, idx, src, axis=0):
    return tgt.at[idx].add(src)

def _segment_sum(src, seg, n):
    return jax.ops.segment_sum(src, seg, n)
kernel_name = 'mk_macaron_d1_jaxref_r8_326379'

def setup_inputs(seed: int=0):
    np.random.seed(seed)
    _w = jnp.asarray

    def _L0_attn_setup():
        import jax, jax.numpy as jnp
        import numpy as np
        H = 16
        G = 4
        MAX_POS = 128
        key = jax.random.key(seed)
        ks = jax.random.split(key, 6)
        B, T, D = (8, 128, 128)
        hd = D // H
        s = 0.02
        return {'x': jax.random.normal(ks[0], (B, T, D), jnp.float32), 'Wq': jax.random.normal(ks[1], (D, D), jnp.float32) * s, 'Wk': jax.random.normal(ks[2], (hd * G, D), jnp.float32) * s, 'Wv': jax.random.normal(ks[3], (hd * G, D), jnp.float32) * s, 'Wo': jax.random.normal(ks[4], (D, D), jnp.float32) * s, 'E': jax.random.normal(ks[5], (2 * MAX_POS - 1, hd), jnp.float32) * s}
    _L0_attn_in = _L0_attn_setup()

    def _L0_ffn_setup():
        import jax, jax.numpy as jnp
        import numpy as np
        D_MODEL = 128
        M = 64
        INNER = 16
        key = jax.random.key(seed)
        ks = jax.random.split(key, 9)

        def init(k, shape, fan_in):
            bound = 1.0 / np.sqrt(fan_in)
            return jax.random.uniform(k, shape, jnp.float32, -bound, bound)
        x = jax.random.normal(ks[0], (16, 512, D_MODEL), dtype=jnp.float32)
        Win = init(ks[1], (D_MODEL, M), D_MODEL)
        bin_ = init(ks[2], (M,), D_MODEL)
        W1 = init(ks[3], (M, INNER), 1)
        b1 = init(ks[4], (M, INNER), 1)
        W2 = init(ks[5], (M, INNER), INNER)
        b2 = init(ks[6], (M,), INNER)
        Wout = init(ks[7], (M, D_MODEL), M)
        bout = init(ks[8], (D_MODEL,), M)
        return {'x': x, 'Win': Win, 'bin_': bin_, 'W1': W1, 'b1': b1, 'W2': W2, 'b2': b2, 'Wout': Wout, 'bout': bout}
    _L0_ffn_in = _L0_ffn_setup()
    _d = {'L0_attn_x': _L0_attn_in['x'], 'L0_attn_Wq': _L0_attn_in['Wq'], 'L0_attn_Wk': _L0_attn_in['Wk'], 'L0_attn_Wv': _L0_attn_in['Wv'], 'L0_attn_Wo': _L0_attn_in['Wo'], 'L0_attn_E': _L0_attn_in['E'], 'L0_ffn_Win': _L0_ffn_in['Win'], 'L0_ffn_bin_': _L0_ffn_in['bin_'], 'L0_ffn_W1': _L0_ffn_in['W1'], 'L0_ffn_b1': _L0_ffn_in['b1'], 'L0_ffn_W2': _L0_ffn_in['W2'], 'L0_ffn_b2': _L0_ffn_in['b2'], 'L0_ffn_Wout': _L0_ffn_in['Wout'], 'L0_ffn_bout': _L0_ffn_in['bout']}
    _x0 = _d['L0_attn_x']
    _d['L0_attn_x'] = jax.random.normal(jax.random.fold_in(jax.random.key(seed), 1), (2, 1024, 128), dtype=_x0.dtype)
    del _x0
    return _d

def reference(L0_attn_x, L0_attn_Wq, L0_attn_Wk, L0_attn_Wv, L0_attn_Wo, L0_attn_E, L0_ffn_Win, L0_ffn_bin_, L0_ffn_W1, L0_ffn_b1, L0_ffn_W2, L0_ffn_b2, L0_ffn_Wout, L0_ffn_bout):

    def _L0_attn_ref(x, Wq, Wk, Wv, Wo, E):
        import jax, jax.numpy as jnp
        import numpy as np
        H = 16
        G = 4
        MAX_POS = 128
        B, T, D = x.shape
        hd = D // H
        r = H // G
        q = (x @ Wq.T).reshape(B, T, H, hd).transpose(0, 2, 1, 3)
        k = (x @ Wk.T).reshape(B, T, G, hd)
        v = (x @ Wv.T).reshape(B, T, G, hd)
        k = jnp.repeat(k, r, axis=2).transpose(0, 2, 1, 3)
        v = jnp.repeat(v, r, axis=2).transpose(0, 2, 1, 3)
        q = q * (1.0 / hd) ** 0.5
        scores = jnp.einsum('bhqd,bhkd->bhqk', q, k)
        pos = jnp.arange(T)
        dist = jnp.clip(pos[None, :] - pos[:, None], -MAX_POS + 1, MAX_POS - 1) + MAX_POS - 1
        R = E[dist]
        bias = jnp.einsum('bhqd,kqd->bhqk', q, R)
        scores = scores + bias
        attn = jax.nn.softmax(scores, axis=-1)
        out = jnp.einsum('bhqk,bhkd->bhqd', attn, v)
        out = out.transpose(0, 2, 1, 3).reshape(B, T, D)
        return out @ Wo.T

    def _L0_ffn_ref(x, Win, bin_, W1, b1, W2, b2, Wout, bout):
        import jax, jax.numpy as jnp
        import numpy as np
        D_MODEL = 128
        M = 64
        INNER = 16
        s = jnp.einsum('btd,dm->btm', x, Win) + bin_
        h = jax.nn.relu(s[..., None] * W1 + b1)
        g = jnp.einsum('btmh,mh->btm', h, W2) + b2
        out = jnp.einsum('btm,md->btd', g, Wout) + bout
        return out
    x = L0_attn_x
    x = x + 0.5 * _L0_ffn_ref(_layernorm(x, axis=-1), L0_ffn_Win, L0_ffn_bin_, L0_ffn_W1, L0_ffn_b1, L0_ffn_W2, L0_ffn_b2, L0_ffn_Wout, L0_ffn_bout)
    x = x + _L0_attn_ref(_layernorm(x, axis=-1), L0_attn_Wq, L0_attn_Wk, L0_attn_Wv, L0_attn_Wo, L0_attn_E)
    x = x + 0.5 * _L0_ffn_ref(_layernorm(x, axis=-1), L0_ffn_Win, L0_ffn_bin_, L0_ffn_W1, L0_ffn_b1, L0_ffn_W2, L0_ffn_b2, L0_ffn_Wout, L0_ffn_bout)
    return x

_drawn_inputs = setup_inputs


def setup_inputs(seed=0):
    import zlib

    import numpy as np

    out = dict(_drawn_inputs(seed))
    spreads = {}
    factors = {'L0_attn_Wq': 8.0,
     'L0_attn_Wk': 8.0,
     'L0_attn_Wv': 8.0,
     'L0_attn_Wo': 8.0,
     'L0_attn_E': 8.0,
     'L0_ffn_bin_': 8.0}
    for name, (base, spread) in spreads.items():
        noise = np.random.default_rng([zlib.crc32(name.encode()), seed]).standard_normal(out[name].shape)
        drawn = base * np.exp(spread * noise) if base else spread * noise
        out[name] = jnp.asarray(drawn.astype(out[name].dtype))
    for name, factor in factors.items():
        out[name] = (out[name] * factor).astype(out[name].dtype)
    return out
```

```python
from contextlib import ExitStack

import concourse.bass as bass
from concourse import mybir

F32 = mybir.dt.float32
BF16 = mybir.dt.bfloat16
ALU = mybir.AluOpType
ACT = mybir.ActivationFunctionType
AX_X = mybir.AxisListType.X

P = 128
B, T, D = 2, 1024, 128
H, G, HD = 16, 4, 8
REACH = 127
NE = 2 * REACH + 1
M, INNER = 64, 16
EPS = 1e-5
NT = B * T // P
QT = T // P
UNITS = B * H // 2
SETS = 4
BANK = 512
WIN = 3 * P
QEW = 256
SLOT = P + T * QEW + P

Q_PART = (0, 0, 1, 0, 2, 1)
K_PART = (0, 1, 0, 2, 0, 1)
KS = HD * len(Q_PART)
KM = KS + 3
HB = 64

S_LEAD = 10
Q_LEAD = 20
SLOTS = UNITS * QT
BODY = SETS * QT
LOOP_FROM = QT
LOOPS = (SLOTS - Q_LEAD - LOOP_FROM) // BODY
LOOP_TO = LOOP_FROM + LOOPS * BODY


def wait(eng, sem, value):
    if isinstance(value, int) and value <= 0:
        return
    eng.wait_ge(sem, value)


def hold(eng, passed):
    eng.sem_inc(passed, 1)


def over_slots(eng, slot):
    for n in range(-Q_LEAD, LOOP_FROM):
        slot((0, n), n)
    with eng.Fori(0, LOOPS) as turn:
        for j in range(LOOP_FROM, LOOP_FROM + BODY):
            slot((turn, j), None)
    for n in range(LOOP_TO, SLOTS + 2):
        slot((0, n), n)


def ahead(at, lead):
    return at[0], at[1] + lead


def slot_no(at, times=1, plus=0):
    return at[0] * (BODY * times) + (at[1] * times + plus)


def unit_no(at, times=1, plus=0):
    return at[0] * (SETS * times) + (at[1] // QT * times + plus)


def key_tile(at):
    return at[1] % QT


def set_of(at):
    return at[1] // QT % SETS


def loads_of(at):
    return at[0] * 80 + 80 * (at[1] // BODY + 1)


def within(static, lead, count=SLOTS):
    return static is None or 0 <= static + lead < count


def macaron_attention(nc, x, Wq_t, Wk_t, Wv_t, Wo_t, E_t, k_shift, Win, b_in, W1, b1, W2, b2,
                      Wout, b_out, out):
    with ExitStack() as ctx:
        def sb(name, shape, dt):
            return ctx.enter_context(nc.sbuf_tensor(name, shape, dt))

        def sem(name):
            return ctx.enter_context(nc.semaphore(name))

        q_rows = nc.dram_tensor("q_rows", [UNITS, 2, KS, T], BF16, kind="Internal").ap()
        k_rows = nc.dram_tensor("k_rows", [B * G, KS, 2, T], BF16, kind="Internal").ap()
        qe_dram = nc.dram_tensor("qe_dram", [SETS * 2, SLOT], F32, kind="Internal").ap()

        ps = ctx.enter_context(nc.psum_tensor("ps", [P, 8, BANK], F32))
        MISC, OUT_BANK, T_BANK, S_BANK = 0, 1, 2, 4

        ident = sb("ident", [P, P], F32)
        x1 = sb("x1", [P, NT, D], F32)
        attn = sb("attn", [P, B, QT, D], F32)
        v_all = sb("v_all", [P, B, G, QT, 32], F32)
        wq = sb("wq", [P, D], F32)
        wk = sb("wk", [P, 2, G * HD], F32)
        wv = sb("wv", [P, G * HD], F32)
        wo = sb("wo", [P, D], F32)
        kshift = sb("kshift", [2 * G * HD, 1], F32)
        win = sb("win", [P, M], F32)
        bin_c = sb("bin_c", [P, 1], F32)
        w1_c = sb("w1_c", [P, INNER], F32)
        b1_c = sb("b1_c", [P, INNER], F32)
        w2_c = sb("w2_c", [P, INNER], F32)
        b2_c = sb("b2_c", [P, 1], F32)
        wout = sb("wout", [P, D], F32)
        bout = sb("bout", [P, D], F32)
        minus_half = sb("minus_half", [P, NT], F32)
        zeros = sb("zeros", [2 * SETS, P], F32)
        e_rev = sb("e_rev", [HD, QEW], F32)
        e_rel = sb("e_rel", [HD, QEW], F32)
        e_rest = sb("e_rest", [HD, 2, QEW], F32)
        e_part = sb("e_part", [HD, 3, QEW], BF16)
        e_rows = sb("e_rows", [P, QEW], BF16)

        bias = sb("bias", [P, SETS, 2, QT, WIN], F32)
        q_set = sb("q_set", [P, SETS, T], BF16)
        k_set = sb("k_set", [P, SETS, 2, T], BF16)
        v_set = sb("v_set", [P, SETS, QT, 32], F32)
        qe_stage = sb("qe_stage", [P, 2, QT, QEW], F32)
        q_last = sb("q_last", [P, 2, QT], F32)
        probs = sb("probs", [P, 8, BANK], F32)
        score_copy = sb("score_copy", [P, 2, WIN], BF16)
        near_max = sb("near_max", [P, 2, 2 * QT], F32)
        far_max = sb("far_max", [P, 2, 2 * QT], F32)
        row_max = sb("row_max", [P, 2 * QT], F32)
        neg_max = sb("neg_max", [2 * QT, 3, P], F32)
        neg_part = sb("neg_part", [2 * QT, 3, P], BF16)
        o_raw = sb("o_raw", [P, BANK], F32)
        o_recip = sb("o_recip", [P, 4, 4], F32)

        room = bias[:].rearrange("p s h t w -> p (s h t w)")
        used = [0]

        def part(cols, dt=F32):
            words = cols if dt == F32 else cols // 2
            v = room[:, used[0]:used[0] + words]
            used[0] += words
            return v if dt == F32 else v.bitcast(dt)

        x_in = part(NT * D).rearrange("p (t d) -> p t d", t=NT)
        xn = part(NT * D).rearrange("p (t d) -> p t d", t=NT)
        xn_t = part(NT * D)
        x_biased = part(NT * D).rearrange("p (t d) -> p t d", t=NT)
        s_t = part(T)
        h_pre = part(T)
        hidden = part(4 * T).rearrange("p (j t) -> p j t", j=4)
        g_t = part(T)
        stats = part(NT * 6).rearrange("p (t s) -> p t s", t=NT)
        mean_var = part(NT * 2).rearrange("p (t s) -> p t s", t=NT)
        var_eps = part(NT)
        rstd = part(NT)
        w2_diag = part(INNER * P).rearrange("p (j n) -> p j n", j=INNER)
        hidden_flat = hidden.rearrange("p j t -> p (j t)")
        q_rest = x_in.rearrange("p t d -> p (t d)")
        k_rest = hidden_flat[0:2 * G * HD, 0:NT * D]
        q32 = hidden_flat[:, NT * D:2 * NT * D]
        k32 = x_biased.rearrange("p t d -> p (t d)")[0:2 * G * HD, :]
        q_split = part(3 * NT * D, BF16).rearrange("p (s t) -> p s t", s=3)
        k_split = part(3 * NT * D, BF16)[0:2 * G * HD, :].rearrange("p (s t) -> p s t", s=3)
        assert used[0] <= SETS * 2 * QT * WIN

        x_loaded = sem("x_loaded")
        weights_loaded = sem("weights_loaded")
        bout_loaded = sem("bout_loaded")
        ident_zero = sem("ident_zero")
        ident_ready = sem("ident_ready")
        consts_ready = sem("consts_ready")
        diag_ready = sem("diag_ready")
        bout_halved = sem("bout_halved")
        e_step = sem("e_step")
        e_placed = sem("e_placed")
        pads_written = sem("pads_written")
        stats_ready = sem("stats_ready")
        mean_ready = sem("mean_ready")
        var_ready = sem("var_ready")
        rstd_ready = sem("rstd_ready")
        xn_ready = sem("xn_ready")
        xnt_in_psum = sem("xnt_in_psum")
        xnt_by_act = sem("xnt_by_act")
        xnt_by_dve = sem("xnt_by_dve")
        x_biased_ready = sem("x_biased_ready")
        s_in_psum = sem("s_in_psum")
        s_by_act = sem("s_by_act")
        s_by_dve = sem("s_by_dve")
        h_by_act = sem("h_by_act")
        h_pre_ready = sem("h_pre_ready")
        h_by_dve = sem("h_by_dve")
        h_used = sem("h_used")
        g_by_act = sem("g_by_act")
        g_by_dve = sem("g_by_dve")
        y_in_psum = sem("y_in_psum")
        x_new = sem("x_new")
        q_in_psum = sem("q_in_psum")
        k_in_psum = sem("k_in_psum")
        v_in_psum = sem("v_in_psum")
        q_scaled = sem("q_scaled")
        k_shifted = sem("k_shifted")
        q_split_step = sem("q_split_step")
        k_split_step = sem("k_split_step")
        v_cleared = sem("v_cleared")
        v_ready = sem("v_ready")
        q_stored = sem("q_stored")
        k_stored = sem("k_stored")
        unit_loaded = [sem(f"unit_loaded{s}") for s in range(SETS)]
        qe_in_psum = sem("qe_in_psum")
        qe_staged = sem("qe_staged")
        qe_stored = [sem(f"qe_stored{h}") for h in range(2)]
        bias_loaded = [sem(f"bias_loaded{h}") for h in range(2)]
        q_last_ready = sem("q_last_ready")
        bias_fixing = sem("bias_fixing")
        bias_ready = sem("bias_ready")
        scores_ready = sem("scores_ready")
        near_done = sem("near_done")
        far_done = sem("far_done")
        row_max_ready = sem("row_max_ready")
        max_in_psum = sem("max_in_psum")
        max_step = sem("max_step")
        max_rows_placed = sem("max_rows_placed")
        st_ready = sem("st_ready")
        exp_done = sem("exp_done")
        pv_done = sem("pv_done")
        o_copied = sem("o_copied")
        o_in_psum = sem("o_in_psum")
        recip_ready = sem("recip_ready")
        attn_ready = sem("attn_ready")
        at_in_psum = sem("at_in_psum")
        at_by_act = sem("at_by_act")
        at_by_dve = sem("at_by_dve")
        proj_in_psum = sem("proj_in_psum")
        x2_ready = sem("x2_ready")
        out_stored = sem("out_stored")
        pool_passed = sem("pool_passed")
        sp_passed = sem("sp_passed")

        x_dram = x.rearrange("(t p) d -> p t d", p=P)
        out_dram = out.rearrange("(t p) d -> p t d", p=P)
        WEIGHTS = 20

        block = ctx.enter_context(nc.Block())

        def near_tiles(qt):
            return [kt for kt in (qt - 1, qt, qt + 1) if 0 <= kt < QT]

        @block.sync
        def _(sp):
            for c in range(2):
                sp.dma_start(x_in[:, 8 * c:8 * c + 8, :], x_dram[:, 8 * c:8 * c + 8, :]).then_inc(x_loaded, 16)
            for dst, src in ((win[:], Win), (wq[:], Wq_t), (wk[:, 0, :], Wk_t), (wk[:, 1, :], Wk_t),
                             (wv[:], Wv_t), (wo[:], Wo_t), (kshift[:], k_shift), (e_rev[:, 0:NE], E_t)):
                sp.dma_start(dst, src).then_inc(weights_loaded, 16)
            for h in range(B):
                rows = slice(M * h, M * h + M)
                for dst, src in ((bin_c, b_in), (w1_c, W1), (b1_c, b1), (w2_c, W2), (b2_c, b2), (wout, Wout)):
                    sp.dma_start(dst[rows, :], src).then_inc(weights_loaded, 16)
            sp.dma_start(bout[:], b_out.partition_broadcast(P)).then_inc(bout_loaded, 16)
            sp.wait_ge(consts_ready, 2)
            sp.dma_start(qe_dram[:, 0:P], zeros[:]).then_inc(pads_written, 16)
            sp.dma_start(qe_dram[:, SLOT - P:SLOT], zeros[:]).then_inc(pads_written, 16)
            sp.wait_ge(e_step, 6)
            for base in (0, HB):
                for r, k in enumerate(K_PART):
                    sp.dma_start(e_rows[base + HD * r:base + HD * r + HD, :], e_part[:, k, :]).then_inc(e_placed, 16)
            for b in range(B):
                for r in range(len(Q_PART)):
                    for v in range(2):
                        if v == 0 and r == 0:
                            sp.wait_ge(k_split_step, 5 * b + 5)
                        sp.dma_start(k_rows[b * G:(b + 1) * G, HD * r:HD * r + HD, v, :],
                                     k_split[v * G * HD:(v + 1) * G * HD, K_PART[r], b * T:(b + 1) * T]
                                     ).then_inc(k_stored, 16)
                for r in range(len(Q_PART)):
                    if r == 0:
                        sp.wait_ge(q_split_step, 5 * b + 5)
                    dst = q_rows[b * QT:(b + 1) * QT, :, HD * r:HD * r + HD, :].rearrange("u h d t -> (u h) d t")
                    sp.dma_start(dst, q_split[:, Q_PART[r], b * T:(b + 1) * T]).then_inc(q_stored, 16)
            sp.wait_ge(k_stored, 16 * 2 * B * len(K_PART))
            sp.wait_ge(q_stored, 16 * B * len(Q_PART))
            sp.wait_ge(pads_written, 32)
            sp.wait_ge(v_ready, NT)

            def load_unit(u, s, k):
                wait(sp, pv_done, QT * (u - SETS) + QT)
                hold(sp, sp_passed)
                uk = u // 2 if isinstance(u, int) else k
                for h in range(2):
                    rows = slice(HB * h, HB * h + KS)
                    sp.dma_start(q_set[rows, s, :], one(q_rows[:, h], u)).then_inc(unit_loaded[s], 16)
                    sp.dma_start(k_set[rows, s, :, :], one(k_rows, uk)).then_inc(unit_loaded[s], 16)
                v_by_unit = v_all[:].rearrange("p b g k c -> p (b g) (k c)")
                src = v_by_unit[:, uk, :] if isinstance(uk, int) else v_by_unit[:, bass.ds(uk, 1), :]
                dst = v_set[:, s, :, :].rearrange("p k c -> p (k c)")
                if not isinstance(uk, int):
                    dst = v_set[:, s:s + 1, :, :].rearrange("p s k c -> p s (k c)")
                sp.dma_start(dst, src).then_inc(unit_loaded[s], 16)

            def one(ap, u):
                if isinstance(u, int):
                    return ap[u]
                v = ap[bass.ds(u, 1)]
                if len(v.shape) == 3:
                    return v.rearrange("o a b -> (o a) b")
                return v.rearrange("o a b c -> (o a) b c")

            def store_and_skew(u, s, h):
                sp.wait_ge(qe_staged, 8 * u + 4 * h + 4)
                hold(sp, sp_passed)
                wait(sp, bias_loaded[h], 16 * u)
                hold(sp, sp_passed)
                z = 2 * s + h
                dst = qe_dram[z, P:P + T * QEW].rearrange("(t p w) -> p t w", p=P, w=QEW)
                sp.dma_start(dst, qe_stage[:, h, :, :]).then_inc(qe_stored[h], 16)
                sp.wait_ge(qe_stored[h], 16 * u + 16)
                hold(sp, sp_passed)
                wait(sp, st_ready, 4 * QT * (u - SETS + 1))
                hold(sp, sp_passed)
                src = bass.AP(qe_dram.tensor, z * SLOT + P - 1, [[QEW - 1, P], [P * QEW, QT], [1, WIN]])
                sp.dma_start(bias[:, s, h, :, :], src).then_inc(bias_loaded[h], 16)

            def max_rows(u, s):
                sp.wait_ge(max_step, 5 * u + 5)
                hold(sp, sp_passed)
                for h in range(2):
                    for i in range(3):
                        dst = q_set[HB * h + KS + i:HB * h + KS + i + 1, s, :]
                        sp.dma_start(dst, neg_part[QT * h:QT * h + QT, i, :]).then_inc(max_rows_placed, 16)

            def step(i, j, static, uk):
                if within(static, 3, UNITS):
                    load_unit(i + 3, (j + 3) % SETS, uk)
                if within(static, 2, UNITS):
                    store_and_skew(i + 2, (j + 2) % SETS, 1)
                if within(static, 1, UNITS):
                    max_rows(i + 1, (j + 1) % SETS)
                if within(static, 3, UNITS):
                    store_and_skew(i + 3, (j + 3) % SETS, 0)

            for i in range(-3, 1):
                step(i, i % SETS, i, None)
            with sp.Fori(0, LOOPS) as turn:
                for j in range(SETS):
                    step(turn * SETS + (1 + j), (1 + j) % SETS, None, turn * 2 + (2 + j // 2))
            for i in range(1 + LOOPS * SETS, UNITS):
                step(i, i % SETS, i, None)

            for c in range(4):
                sp.wait_ge(x_new, 4 + c + 1)
                sp.dma_start(out_dram[:, 4 * c:4 * c + 4, :], xn[:, 4 * c:4 * c + 4, :]).then_inc(out_stored, 16)
            sp.wait_ge(out_stored, 64)

        @block.gpsimd
        def _(pool):
            pool.memset(ident[:], 0.0).then_inc(ident_zero, 1)
            pool.wait_ge(ident_zero, 1)
            pool.affine_select(out=ident[:], in_=ident[:], compare_op=ALU.not_equal, fill=1.0, base=0,
                               pattern=[[-1, P]], channel_multiplier=1).then_inc(ident_ready, 1)
            pool.memset(minus_half[:], -0.5).then_inc(consts_ready, 1)
            pool.memset(zeros[:], 0.0).then_inc(consts_ready, 1)
            pool.memset(k_set[:], 1.0).then_inc(consts_ready, 1)
            pool.memset(v_all[:], 0.0).then_inc(v_cleared, 1)
            pool.wait_ge(v_cleared, 1)
            pool.memset(v_all[:, :, :, :, HD:HD + 1], 1.0).then_inc(v_cleared, 1)
            pool.wait_ge(bout_loaded, 16)
            pool.tensor_scalar(bout[:], bout[:], 0.5, None, ALU.mult).then_inc(bout_halved, 1)
            pool.wait_ge(bout_halved, 1)
            pool.wait_ge(x_loaded, 32)
            bout_all = bout[:].rearrange("p (o d) -> p o d", o=1).broadcast_to([P, NT, D])

            def rstd_of(f):
                pool.wait_ge(var_ready, f + 1)
                pool.tensor_tensor(rstd, var_eps, minus_half[:], ALU.pow).then_inc(rstd_ready, 1)

            pool.tensor_tensor(x_biased, x_in, bout_all, ALU.add).then_inc(x_biased_ready, 1)
            rstd_of(0)
            pool.wait_ge(weights_loaded, 16 * WEIGHTS)
            pool.wait_ge(ident_ready, 1)
            for j in range(INNER):
                pool.tensor_scalar(w2_diag[:, j, :], ident[:], w2_c[:, j:j + 1], None, ALU.mult).then_inc(diag_ready, 1)
            rstd_of(1)

            for b in range(B):
                cols = slice(b * T, (b + 1) * T)
                kr = k_rest[:, cols]
                kk = k32[:, cols]
                pool.wait_ge(k_shifted, b + 1)
                pool.tensor_copy(k_split[:, 0, cols], kk).then_inc(k_split_step, 1)
                pool.wait_ge(k_split_step, 5 * b + 1)
                pool.tensor_tensor(kr, kk, k_split[:, 0, cols], ALU.subtract).then_inc(k_split_step, 1)
                pool.wait_ge(k_split_step, 5 * b + 2)
                pool.tensor_copy(k_split[:, 1, cols], kr).then_inc(k_split_step, 1)
                pool.wait_ge(k_split_step, 5 * b + 3)
                pool.tensor_tensor(kk, kr, k_split[:, 1, cols], ALU.subtract).then_inc(k_split_step, 1)
                pool.wait_ge(k_split_step, 5 * b + 4)
                pool.tensor_copy(k_split[:, 2, cols], kk).then_inc(k_split_step, 1)

            def keep_last(u, h):
                pool.wait_ge(qe_staged, 8 * u + 4 * h + 4)
                wait(pool, bias_fixing, 2 * (2 * (u - 1) + h + 1))
                hold(pool, pool_passed)
                pool.tensor_copy(q_last[:, h, :], qe_stage[:, h, :, NE - 1:NE].rearrange("p t o -> p (t o)")
                                 ).then_inc(q_last_ready, 1)

            def fix(u, s, h):
                head = 2 * u + h
                left = bias[:, s, h, :, 0:P]
                right = bias[:, s, h, :, 2 * P:WIN]
                pool.wait_ge(bias_loaded[h], 16 * u + 16)
                hold(pool, pool_passed)
                pool.affine_select(out=left, in_=left, compare_op=ALU.is_ge, fill=0.0, base=-1,
                                   pattern=[[0, QT], [1, P]], channel_multiplier=-1).then_inc(bias_fixing, 1)
                pool.wait_ge(q_last_ready, head + 1)
                last = q_last[:, h, :].rearrange("p (t o) -> p t o", o=1).broadcast_to([P, QT, P])
                pool.tensor_tensor(right, right, last, ALU.subtract).then_inc(bias_fixing, 1)
                pool.wait_ge(bias_fixing, 2 * head + 2)
                hold(pool, pool_passed)
                pool.affine_select(out=right, in_=right, compare_op=ALU.is_ge, fill=0.0, base=-1,
                                   pattern=[[0, QT], [-1, P]], channel_multiplier=1).then_inc(bias_ready, 1)

            def step(i, j, static):
                if within(static, 2, UNITS):
                    keep_last(i + 2, 1)
                    fix(i + 2, (j + 2) % SETS, 1)
                if within(static, 3, UNITS):
                    keep_last(i + 3, 0)
                    fix(i + 3, (j + 3) % SETS, 0)

            for i in range(-3, 1):
                step(i, i % SETS, i)
            with pool.Fori(0, LOOPS) as turn:
                for j in range(SETS):
                    step(turn * SETS + (1 + j), (1 + j) % SETS, None)
            for i in range(1 + LOOPS * SETS, UNITS):
                step(i, i % SETS, i)

            pool.wait_ge(st_ready, 4 * SLOTS)
            for j in range(INNER):
                pool.tensor_scalar(w2_diag[:, j, :], ident[:], w2_c[:, j:j + 1], None, ALU.mult).then_inc(diag_ready, 1)
            pool.wait_ge(x2_ready, 4)
            pool.tensor_tensor(x_biased, x1[:], bout_all, ALU.add).then_inc(x_biased_ready, 1)
            rstd_of(2)

        @block.scalar
        def _(act):
            def xn_t_copy(f):
                for c in (0, 2):
                    act.wait_ge(xnt_in_psum, 4 * f + c + 1)
                    act.copy(xn_t[:, c * BANK:(c + 1) * BANK], ps[:, c, :]).then_inc(xnt_by_act, 1)

            def ffn(f):
                act.wait_ge(s_in_psum, f + 1)
                act.activation(s_t[:, 0:BANK], ps[:, 4, :], ACT.Identity, bias=bin_c[:, 0:1]).then_inc(s_by_act, 1)
                act.wait_ge(s_by_act, f + 1)
                act.wait_ge(s_by_dve, f + 1)
                for j in range(0, INNER, 2):
                    n = INNER * f + j
                    if n >= 4:
                        act.wait_ge(h_used, n - 3)
                    act.activation(hidden[:, j % 4, :], s_t, ACT.Relu, bias=b1_c[:, j:j + 1],
                                   scale=w1_c[:, j:j + 1]).then_inc(h_by_act, 1)
                act.wait_ge(h_used, INNER * (f + 1))
                act.activation(g_t[:, 0:BANK], ps[:, 6, :], ACT.Identity, bias=b2_c[:, 0:1]).then_inc(g_by_act, 1)

            act.wait_ge(weights_loaded, 16 * WEIGHTS)
            xn_t_copy(0)
            ffn(0)
            xn_t_copy(1)
            for c in range(4):
                act.wait_ge(q_in_psum, c + 1)
                act.mul(q32[:, c * BANK:(c + 1) * BANK], ps[:, c, :], (1.0 / HD) ** 0.5).then_inc(q_scaled, 1)

            def stage_qe(at):
                h, pair = key_tile(at) // 4, key_tile(at) % 4
                act.wait_ge(qe_in_psum, slot_no(at, 1, 1))
                wait(act, qe_stored[h], unit_no(at, 16))
                wait(act, q_last_ready, unit_no(at, 2, h - 1))
                act.copy(qe_stage[:, h, 2 * pair:2 * pair + 2, :].rearrange("p t w -> p (t w)"),
                         ps[:, MISC, :]).then_inc(qe_staged, 1)

            def slot(at, static):
                if within(static, Q_LEAD):
                    stage_qe(ahead(at, Q_LEAD))
                if within(static, 0):
                    for t in range(4):
                        act.wait_ge(st_ready, slot_no(at, 4, t + 1))
                        if t == 0:
                            wait(act, pv_done, slot_no(at, 1, -1))
                        act.activation(probs[:, 4 * (at[1] % 2) + t, :], ps[:, T_BANK + t % 2, :],
                                       ACT.Exp).then_inc(exp_done, 1)

            over_slots(act, slot)
            for c in (0, 2):
                act.wait_ge(at_in_psum, c + 1)
                act.copy(xn_t[:, c * BANK:(c + 1) * BANK], ps[:, c, :]).then_inc(at_by_act, 1)
            xn_t_copy(2)
            ffn(1)

        @block.vector
        def _(dve):
            dve.memset(o_recip[:], 1.0).then_inc(attn_ready, 2)
            dve.wait_ge(weights_loaded, 16 * WEIGHTS)
            dve.tensor_copy(e_rev[:, NE:QEW], e_rev[:, NE - 1:NE]).then_inc(e_step, 1)
            dve.wait_ge(e_step, 1)
            dve.tensor_scalar(e_rel[:], e_rev[:], e_rev[:, 0:1], None, ALU.subtract).then_inc(e_step, 1)
            dve.wait_ge(e_step, 2)
            dve.tensor_copy(e_part[:, 0, :], e_rel[:]).then_inc(e_step, 1)
            dve.wait_ge(e_step, 3)
            dve.tensor_tensor(e_rest[:, 0, :], e_rel[:], e_part[:, 0, :], ALU.subtract).then_inc(e_step, 1)
            dve.wait_ge(e_step, 4)
            dve.tensor_copy(e_part[:, 1, :], e_rest[:, 0, :]).then_inc(e_step, 1)
            dve.wait_ge(e_step, 5)
            dve.tensor_tensor(e_part[:, 2, :], e_rest[:, 0, :], e_part[:, 1, :], ALU.subtract).then_inc(e_step, 1)

            def layer_norm(f, src):
                for t in range(NT):
                    dve.bn_stats(stats[:, t, :], src[:, t, :]).then_inc(stats_ready, 1)
                for t in range(NT):
                    dve.wait_ge(stats_ready, NT * f + t + 1)
                    dve.bn_aggr(mean_var[:, t, :], stats[:, t, :]).then_inc(mean_ready, 1)
                dve.wait_ge(mean_ready, NT * (f + 1))
                dve.tensor_scalar(var_eps, mean_var[:, :, 1:2].rearrange("p t o -> p (t o)"), EPS, None,
                                  ALU.add).then_inc(var_ready, 1)
                dve.wait_ge(rstd_ready, f + 1)
                for t in range(NT):
                    dve.tensor_scalar(xn[:, t, :], src[:, t, :], mean_var[:, t, 0:1], rstd[:, t:t + 1],
                                      ALU.subtract, ALU.mult).then_inc(xn_ready, 1)
                for c in (1, 3):
                    dve.wait_ge(xnt_in_psum, 4 * f + c + 1)
                    dve.tensor_copy(xn_t[:, c * BANK:(c + 1) * BANK], ps[:, c, :]).then_inc(xnt_by_dve, 1)

            def ffn(f, dst):
                dve.wait_ge(s_in_psum, f + 1)
                dve.tensor_scalar(s_t[:, BANK:T], ps[:, 5, :], bin_c[:, 0:1], None, ALU.add).then_inc(s_by_dve, 1)
                dve.wait_ge(s_by_act, f + 1)
                dve.wait_ge(s_by_dve, f + 1)
                for j in range(1, INNER, 2):
                    n = INNER * f + j
                    odd = n // 2
                    if odd:
                        dve.wait_ge(h_by_dve, odd)
                    dve.tensor_scalar(h_pre, s_t, w1_c[:, j:j + 1], b1_c[:, j:j + 1], ALU.mult,
                                      ALU.add).then_inc(h_pre_ready, 1)
                    dve.wait_ge(h_pre_ready, odd + 1)
                    if n >= 4:
                        dve.wait_ge(h_used, n - 3)
                    dve.tensor_scalar(hidden[:, j % 4, :], h_pre, 0.0, None, ALU.max).then_inc(h_by_dve, 1)
                dve.wait_ge(h_used, INNER * (f + 1))
                dve.tensor_scalar(g_t[:, BANK:T], ps[:, 7, :], b2_c[:, 0:1], None, ALU.add).then_inc(g_by_dve, 1)
                dve.wait_ge(x_biased_ready, f + 1)
                for c in range(4):
                    dve.wait_ge(y_in_psum, 4 * f + c + 1)
                    dve.scalar_tensor_tensor(out=dst[:, 4 * c:4 * c + 4, :].rearrange("p t d -> p (t d)"),
                                             in0=ps[:, c, :], scalar=0.5,
                                             in1=x_biased[:, 4 * c:4 * c + 4, :].rearrange("p t d -> p (t d)"),
                                             op0=ALU.mult, op1=ALU.add).then_inc(x_new, 1)

            dve.wait_ge(x_loaded, 32)
            layer_norm(0, x_in)
            ffn(0, x1)
            dve.wait_ge(x_new, 4)
            layer_norm(1, x1)
            for b in range(B):
                for c in (2 * b, 2 * b + 1):
                    dve.wait_ge(k_in_psum, c + 1)
                    last = dve.tensor_scalar(k32[:, c * BANK:(c + 1) * BANK], ps[0:2 * G * HD, 4 + c, :],
                                             kshift[:, 0:1], None, ALU.add)
                last.then_inc(k_shifted, 1)
            for b in range(B):
                cols = slice(b * T, (b + 1) * T)
                dve.wait_ge(q_scaled, 2 * b + 2)
                dve.tensor_copy(q_split[:, 0, cols], q32[:, cols]).then_inc(q_split_step, 1)
                dve.wait_ge(q_split_step, 5 * b + 1)
                dve.tensor_tensor(q_rest[:, cols], q32[:, cols], q_split[:, 0, cols],
                                  ALU.subtract).then_inc(q_split_step, 1)
                dve.wait_ge(q_split_step, 5 * b + 2)
                dve.tensor_copy(q_split[:, 1, cols], q_rest[:, cols]).then_inc(q_split_step, 1)
                dve.wait_ge(q_split_step, 5 * b + 3)
                dve.tensor_tensor(q32[:, cols], q_rest[:, cols], q_split[:, 1, cols],
                                  ALU.subtract).then_inc(q_split_step, 1)
                dve.wait_ge(q_split_step, 5 * b + 4)
                dve.tensor_copy(q_split[:, 2, cols], q32[:, cols]).then_inc(q_split_step, 1)
            dve.wait_ge(v_in_psum, 1)
            dve.wait_ge(v_cleared, 2)
            for t in range(NT):
                dve.tensor_copy(v_all[:, t // QT, :, t % QT, 0:HD],
                                ps[:, MISC, 32 * t:32 * t + 32].rearrange("p (g d) -> p g d", g=G)
                                ).then_inc(v_ready, 1)

            def score_max(at, which):
                s, tile = set_of(at), 2 * key_tile(at) + which
                h, qt, par = tile // QT, tile % QT, s % 2
                near = len(near_tiles(qt)) * P
                first = (near_tiles(qt)[0] - qt + 1) * P
                base = S_BANK + 2 * which
                cols = ps[:, base:base + 2, :].rearrange("p b n -> p (b n)")
                if qt == 0:
                    dve.wait_ge(bias_ready, unit_no(at, 2, h + 1))
                dve.wait_ge(scores_ready, slot_no(at, 2, which + 1))
                wait(dve, near_done, slot_no(at, 2, which - 1))
                dve.tensor_reduce(far_max[:, par, tile:tile + 1], cols[:, near:2 * BANK], AX_X,
                                  ALU.max).then_inc(far_done, 1)
                dve.tensor_tensor_reduce(score_copy[:, tile % 2, 0:near],
                                         cols[:, 0:near],
                                         bias[:, s, h, qt, first:first + near], 1.0, -3.0e38, ALU.add, ALU.max,
                                         near_max[:, par, tile:tile + 1]).then_inc(near_done, 1)

            def unit_max(at):
                par = set_of(at) % 2
                dve.wait_ge(near_done, unit_no(at, 16, 16))
                dve.wait_ge(far_done, unit_no(at, 16, 16))
                dve.tensor_tensor(row_max[:], near_max[:, par, :], far_max[:, par, :], ALU.max).then_inc(row_max_ready, 1)

            def max_parts(at):
                dve.wait_ge(max_in_psum, unit_no(at, 1, 1))
                wait(dve, max_rows_placed, unit_no(at, 96))
                dve.tensor_scalar(neg_max[:, 0, :], ps[0:2 * QT, MISC, 0:P], -1.0, None, ALU.mult).then_inc(max_step, 1)
                dve.wait_ge(max_step, unit_no(at, 5, 1))
                dve.tensor_copy(neg_part[:, 0, :], neg_max[:, 0, :]).then_inc(max_step, 1)
                dve.wait_ge(max_step, unit_no(at, 5, 2))
                dve.tensor_tensor(neg_max[:, 1, :], neg_max[:, 0, :], neg_part[:, 0, :], ALU.subtract).then_inc(max_step, 1)
                dve.wait_ge(max_step, unit_no(at, 5, 3))
                dve.tensor_copy(neg_part[:, 1, :], neg_max[:, 1, :]).then_inc(max_step, 1)
                dve.wait_ge(max_step, unit_no(at, 5, 4))
                dve.tensor_tensor(neg_part[:, 2, :], neg_max[:, 1, :], neg_part[:, 1, :], ALU.subtract).then_inc(max_step, 1)

            def copy_out(at):
                dve.wait_ge(pv_done, unit_no(at, QT, QT))
                dve.wait_ge(attn_ready, unit_no(at, 2, 2))
                dve.tensor_copy(o_raw[:], ps[:, OUT_BANK, :]).then_inc(o_copied, 1)

            def normalise(at):
                dve.wait_ge(o_in_psum, unit_no(at, 1, 1))
                o = ps[:, MISC, :].rearrange("p (c h f j) -> p c h f j", c=4, h=2, f=2)
                dve.reciprocal(o_recip[:].rearrange("p c (a o) -> p c a o", o=1),
                               ps[:, MISC, :].rearrange("p (c a j) -> p c a j", c=4, a=4)[:, :, :, HD:HD + 1]
                               ).then_inc(recip_ready, 1)
                dve.wait_ge(recip_ready, unit_no(at, 1, 1))
                u = unit_no(at)
                r = o_recip[:].rearrange("p c (h f o) -> p c h f o", h=2, f=2)
                for f in range(2):
                    dst = attn[:, bass.ds(u // QT, 1), 4 * f:4 * f + 4, bass.ds(u % QT * (2 * HD), 2 * HD)]
                    dst = dst.rearrange("p o c j -> p (o c) j")
                    dve.tensor_tensor(dst.rearrange("p c (h d) -> p c h d", h=2), o[:, :, :, f, 0:HD],
                                      r[:, :, :, f, :].broadcast_to([P, 4, 2, HD]), ALU.mult).then_inc(attn_ready, 1)

            def slot(at, static):
                if key_tile(at) == 1 and within(static, -QT):
                    copy_out(ahead(at, -QT))
                s_at = ahead(at, S_LEAD)
                if within(static, S_LEAD):
                    score_max(s_at, 0)
                    score_max(s_at, 1)
                    if key_tile(s_at) == QT - 1:
                        unit_max(s_at)
                if key_tile(at) == QT - 2 and within(static, 2):
                    max_parts(ahead(at, 2))
                if key_tile(at) == 1 and within(static, -QT):
                    normalise(ahead(at, -QT))

            over_slots(dve, slot)

            for c in (1, 3):
                dve.wait_ge(at_in_psum, c + 1)
                dve.tensor_copy(xn_t[:, c * BANK:(c + 1) * BANK], ps[:, c, :]).then_inc(at_by_dve, 1)
            for c in range(4):
                dve.wait_ge(proj_in_psum, c + 1)
                cols = x1[:, 4 * c:4 * c + 4, :].rearrange("p t d -> p (t d)")
                dve.tensor_tensor(cols, ps[:, 4 + c, :], cols, ALU.add).then_inc(x2_ready, 1)
            dve.wait_ge(x2_ready, 4)
            layer_norm(2, x1[:])
            ffn(1, xn)

        @block.tensor
        def _(pe):
            def transposes(f):
                for c in range(4):
                    for t in range(4 * c, 4 * c + 4):
                        pe.wait_ge(xn_ready, NT * f + t + 1)
                        last = pe.transpose(ps[:, c, P * (t % 4):P * (t % 4) + P], xn[:, t, :], ident[:])
                    last.then_inc(xnt_in_psum, 1)
                pe.wait_ge(xnt_by_act, 2 * f + 2)
                pe.wait_ge(xnt_by_dve, 2 * f + 2)

            def ffn(f):
                for b in range(B):
                    for c in range(2):
                        cols = slice(b * T + c * BANK, b * T + (c + 1) * BANK)
                        last = pe.matmul(ps[M * b:M * b + M, 4 + c, :], win[:], xn_t[:, cols], start=True, stop=True)
                last.then_inc(s_in_psum, 1)
                pe.wait_ge(diag_ready, INNER * (f + 1))
                for j in range(INNER):
                    if j % 2 == 0:
                        pe.wait_ge(h_by_act, INNER // 2 * f + j // 2 + 1)
                    else:
                        pe.wait_ge(h_by_dve, INNER // 2 * f + j // 2 + 1)
                    for c in range(2):
                        last = pe.matmul(ps[:, 6 + c, :], w2_diag[:, j, :], hidden[:, j % 4, c * BANK:(c + 1) * BANK],
                                         start=(j == 0), stop=(j == INNER - 1))
                    last.then_inc(h_used, 1)
                pe.wait_ge(g_by_act, f + 1)
                pe.wait_ge(g_by_dve, f + 1)
                for t in range(NT):
                    rows = slice(M * (t // QT), M * (t // QT) + M)
                    last = pe.matmul(ps[:, t // 4, P * (t % 4):P * (t % 4) + P],
                                     g_t[rows, P * (t % QT):P * (t % QT) + P], wout[rows, :], start=True, stop=True)
                    if t % 4 == 3:
                        last.then_inc(y_in_psum, 1)

            pe.wait_ge(ident_ready, 1)
            transposes(0)
            pe.wait_ge(weights_loaded, 16 * WEIGHTS)
            ffn(0)
            pe.wait_ge(x_new, 4)
            transposes(1)
            for c in range(4):
                cols = slice(c * BANK, (c + 1) * BANK)
                pe.matmul(ps[:, c, :], wq[:], xn_t[:, cols], start=True, stop=True).then_inc(q_in_psum, 1)
                pe.matmul(ps[0:2 * G * HD, 4 + c, :], wk[:].rearrange("p v c -> p (v c)"), xn_t[:, cols],
                          start=True, stop=True).then_inc(k_in_psum, 1)
            pe.wait_ge(q_scaled, 1)
            for t in range(NT):
                last = pe.matmul(ps[:, MISC, 32 * t:32 * t + 32], xn_t[:, P * t:P * t + P], wv[:], start=True, stop=True)
            last.then_inc(v_in_psum, 1)
            pe.wait_ge(q_scaled, 4)
            pe.wait_ge(k_shifted, 2)
            pe.wait_ge(v_ready, NT)
            pe.wait_ge(e_placed, 16 * 2 * len(K_PART))
            pe.wait_ge(consts_ready, 3)

            def qe(at):
                s, h, pair = set_of(at), key_tile(at) // 4, key_tile(at) % 4
                if key_tile(at) == 0:
                    pe.wait_ge(unit_loaded[s], loads_of(at))
                wait(pe, qe_staged, slot_no(at))
                rows = slice(HB * h, HB * h + KS)
                for i in range(2):
                    qt = 2 * pair + i
                    last = pe.matmul(ps[:, MISC, QEW * i:QEW * i + QEW], q_set[rows, s, P * qt:P * qt + P],
                                     e_rows[rows, :], start=True, stop=True)
                last.then_inc(qe_in_psum, 1)

            def scores(at, which):
                s, tile = set_of(at), 2 * key_tile(at) + which
                h, qt = tile // QT, tile % QT
                near = near_tiles(qt)
                order = near + [kt for kt in range(QT) if kt not in near]
                wait(pe, near_done, slot_no(at, 2, which - 1))
                wait(pe, far_done, slot_no(at, 2, which - 1))
                rows = slice(HB * h, HB * h + KS)
                at = 0
                while at < QT:
                    n = 1
                    while (at + n < QT and order[at + n] == order[at] + n and (at + n) % 4
                           and (order[at + n] > qt) == (order[at] > qt)):
                        n += 1
                    kt = order[at]
                    last = pe.matmul(ps[:, S_BANK + 2 * which + at // 4, P * (at % 4):P * (at % 4 + n)],
                                     q_set[rows, s, P * qt:P * qt + P],
                                     k_set[rows, s, int(kt > qt), P * kt:P * (kt + n)], start=True, stop=True)
                    at += n
                last.then_inc(scores_ready, 1)

            def exponents(at, t):
                s, kt = set_of(at), key_tile(at)
                h, half = t // 2, t % 2
                rows = slice(HB * h, HB * h + KM)
                bank = T_BANK + t % 2
                wait(pe, exp_done, slot_no(at, 4, t - 1))
                first = True
                for i in range(4):
                    qt = 4 * half + i
                    if abs(qt - kt) <= 1:
                        w = (kt - qt + 1) * P
                        pe.matmul(ps[:, bank, P * i:P * i + P], bias[:, s, h, qt, w:w + P], ident[:],
                                  is_transpose=True, start=first, stop=False, skip_group_check=True)
                        first = False
                cut = min(max(kt - 4 * half, 0), 4)
                for var, a, b in ((1, 0, cut), (0, cut, 4)):
                    if a < b:
                        last = pe.matmul(ps[:, bank, P * a:P * b], k_set[rows, s, var, P * kt:P * kt + P],
                                         q_set[rows, s, P * (4 * half + a):P * (4 * half + b)],
                                         start=first, stop=True, skip_group_check=True)
                        first = False
                last.then_inc(st_ready, 1)

            def weigh(at):
                s, kt = set_of(at), key_tile(at)
                if kt == 0:
                    wait(pe, o_copied, unit_no(at))
                pe.wait_ge(exp_done, slot_no(at, 4, 4))
                for t in range(4):
                    last = pe.matmul(ps[32 * t:32 * t + 32, OUT_BANK, :], v_set[:, s, kt, :],
                                     probs[:, 4 * (at[1] % 2) + t, :], start=(kt == 0), stop=(kt == QT - 1))
                last.then_inc(pv_done, 1)

            def max_to_rows(at):
                pe.wait_ge(row_max_ready, unit_no(at, 1, 1))
                pe.transpose(ps[0:2 * QT, MISC, 0:P], row_max[:], ident[:]).then_inc(max_in_psum, 1)

            def outputs_to_rows(at):
                pe.wait_ge(o_copied, unit_no(at, 1, 1))
                for c in range(4):
                    last = pe.transpose(ps[:, MISC, P * c:P * c + P], o_raw[:, P * c:P * c + P], ident[:])
                last.then_inc(o_in_psum, 1)

            def misc_free(at, static):
                if within(static, Q_LEAD):
                    pe.wait_ge(qe_staged, slot_no(at, 1, Q_LEAD + 1))

            def slot(at, static):
                kt = key_tile(at)
                s_at = ahead(at, S_LEAD)
                if kt == QT - 1 and within(static, 1):
                    pe.wait_ge(max_step, unit_no(ahead(at, 1), 5, 1))
                if kt == 2 and within(static, -QT):
                    pe.wait_ge(attn_ready, unit_no(ahead(at, -QT), 2, 4))
                if within(static, Q_LEAD):
                    qe(ahead(at, Q_LEAD))
                if within(static, 0):
                    if kt == 0:
                        pe.wait_ge(max_rows_placed, unit_no(at, 96, 96))
                        pe.wait_ge(bias_ready, unit_no(at, 2, 2))
                    exponents(at, 0)
                if within(static, S_LEAD):
                    if key_tile(s_at) == 0:
                        pe.wait_ge(unit_loaded[set_of(s_at)], loads_of(s_at))
                    scores(s_at, 0)
                if within(static, 0):
                    exponents(at, 1)
                    exponents(at, 2)
                if within(static, S_LEAD):
                    scores(s_at, 1)
                if kt == QT - 2 and within(static, 2):
                    misc_free(at, static)
                    max_to_rows(ahead(at, 2))
                if kt == 1 and within(static, -QT):
                    misc_free(at, static)
                    outputs_to_rows(ahead(at, -QT))
                if within(static, 0):
                    exponents(at, 3)
                if within(static, -1):
                    weigh(ahead(at, -1))

            over_slots(pe, slot)

            pe.wait_ge(attn_ready, 2 * UNITS + 2)
            for c in range(4):
                for t in range(4 * c, 4 * c + 4):
                    b, qt = t // QT, t % QT
                    last = pe.transpose(ps[:, c, P * (t % 4):P * (t % 4) + P],
                                        attn[:, b, qt, :], ident[:])
                last.then_inc(at_in_psum, 1)
            pe.wait_ge(at_by_act, 2)
            pe.wait_ge(at_by_dve, 2)
            for t in range(NT):
                last = pe.matmul(ps[:, 4 + t // 4, P * (t % 4):P * (t % 4) + P], xn_t[:, P * t:P * t + P], wo[:],
                                 start=True, stop=True)
                if t % 4 == 3:
                    last.then_inc(proj_in_psum, 1)
            transposes(2)
            ffn(1)


def kernel(L0_attn_x, L0_attn_Wq, L0_attn_Wk, L0_attn_Wv, L0_attn_Wo, L0_attn_E, L0_ffn_Win, L0_ffn_bin_,
           L0_ffn_W1, L0_ffn_b1, L0_ffn_W2, L0_ffn_b2, L0_ffn_Wout, L0_ffn_bout):
    import numpy as np
    import concourse.bacc as bacc
    from concourse import mybir as my
    from concourse.bass_utils import run_bass_kernel_spmd

    E = np.asarray(L0_attn_E)
    arrays = {
        "x": np.asarray(L0_attn_x).reshape(B * T, D),
        "Wq_t": np.asarray(L0_attn_Wq).T,
        "Wk_t": np.asarray(L0_attn_Wk).T,
        "Wv_t": np.asarray(L0_attn_Wv).T,
        "Wo_t": np.asarray(L0_attn_Wo).T,
        "E_t": E[::-1].T,
        "k_shift": np.concatenate([np.tile(E[NE - 1], G), np.tile(E[0], G)])[:, None],
        "Win": L0_ffn_Win,
        "b_in": np.asarray(L0_ffn_bin_)[:, None],
        "W1": L0_ffn_W1,
        "b1": L0_ffn_b1,
        "W2": L0_ffn_W2,
        "b2": np.asarray(L0_ffn_b2)[:, None],
        "Wout": L0_ffn_Wout,
        "b_out": L0_ffn_bout,
    }
    nc = bacc.Bacc("TRN2", target_bir_lowering=False, num_devices=1)
    feeds, args = {}, []
    for name, a in arrays.items():
        a = np.ascontiguousarray(a)
        feeds[f"in_{name}"] = a
        args.append(nc.dram_tensor(f"in_{name}", a.shape, my.dt.from_np(a.dtype), kind="ExternalInput").ap())
    args.append(nc.dram_tensor("out", [B * T, D], F32, kind="ExternalOutput").ap())
    macaron_attention(nc, *args)
    r = run_bass_kernel_spmd(nc, [feeds], core_ids=[0])
    return r.results[0]["out"].reshape(B, T, D)
```

```python
from contextlib import ExitStack

import concourse.bass as bass
from concourse import mybir

F32 = mybir.dt.float32
BF16 = mybir.dt.bfloat16
ALU = mybir.AluOpType
ACT = mybir.ActivationFunctionType
AX_X = mybir.AxisListType.X

P = 128
B, T, D = 2, 1024, 128
H, G, HD = 16, 4, 8
REACH = 127
NE = 2 * REACH + 1
M, INNER = 64, 16
EPS = 1e-5
NT = B * T // P
QT = T // P
UNITS = B * H // 2
SETS = 4
BANK = 512
WIN = 3 * P
QEW = 256
SLOT = P + T * QEW + P

Q_PART = (0, 0, 0, 1, 1, 2)
K_PART = (0, 1, 2, 0, 1, 0)
KS = HD * len(Q_PART)
KM = KS + 3
QD = 3 * HD + 3
HB = 64

PE_UNITS, ACT_UNITS = 8, 4
OWN_UNITS = INNER - PE_UNITS - ACT_UNITS
ACT_ORDER = (0, 8, 1, 2, 9, 3, 4, 10, 5, 6, 11, 7)
assert sorted(ACT_ORDER) == list(range(PE_UNITS + ACT_UNITS)) and OWN_UNITS == ACT_UNITS

S_LEAD = 12
M_LEAD = S_LEAD - 8
Q_LEAD = 20
Q_FIRST = QT + QT // 2
SLOTS = UNITS * QT
BODY = SETS * QT
LOOP_FROM = QT
LOOPS = (SLOTS - Q_LEAD - LOOP_FROM) // BODY
LOOP_TO = LOOP_FROM + LOOPS * BODY


def wait(eng, sem, value):
    if isinstance(value, int) and value <= 0:
        return
    eng.wait_ge(sem, value)


def hold(eng, passed):
    eng.sem_inc(passed, 1)


def over_slots(eng, slot):
    for n in range(-Q_LEAD, LOOP_FROM):
        slot((0, n), n)
    with eng.Fori(0, LOOPS) as turn:
        for j in range(LOOP_FROM, LOOP_FROM + BODY):
            slot((turn, j), None)
    for n in range(LOOP_TO, SLOTS + 2):
        slot((0, n), n)


def ahead(at, lead):
    return at[0], at[1] + lead


def slot_no(at, times=1, plus=0):
    return at[0] * (BODY * times) + (at[1] * times + plus)


def unit_no(at, times=1, plus=0):
    return at[0] * (SETS * times) + (at[1] // QT * times + plus)


def key_tile(at):
    return at[1] % QT


def set_of(at):
    return at[1] // QT % SETS


def loads_of(at, loads):
    return at[0] * (16 * loads) + 16 * loads * (at[1] // BODY + 1)


def within(static, lead, count=SLOTS):
    return static is None or 0 <= static + lead < count


def macaron_attention(nc, x, w_rows, w_channels, E_t, e_masks, k_shift, b_out, out):
    with ExitStack() as ctx:
        def sb(name, shape, dt):
            return ctx.enter_context(nc.sbuf_tensor(name, shape, dt))

        def sem(name):
            return ctx.enter_context(nc.semaphore(name))

        q_parts = nc.dram_tensor("q_parts", [2 * UNITS, QD, T], BF16, kind="Internal").ap()
        k_parts = nc.dram_tensor("k_parts", [B, 2 * G, 3 * HD, T], BF16, kind="Internal").ap()
        qe_dram = nc.dram_tensor("qe_dram", [SETS * 2, SLOT], F32, kind="Internal").ap()

        ps = ctx.enter_context(nc.psum_tensor("ps", [P, 8, BANK], F32))
        MISC, OUT_BANK, T_BANK, S_BANK = 0, 1, 2, 4

        ident = sb("ident", [P, P], F32)
        x1 = sb("x1", [P, NT, D], F32)
        attn = sb("attn", [P, QT, B * D], F32)
        v_all = sb("v_all", [P, B, G, QT, 32], F32)
        w_row = sb("w_row", [P, M + D + 3 * G * HD + D], F32)
        at_q, at_k, at_v, at_o = M, M + D, M + D + 2 * G * HD, M + D + 3 * G * HD
        win, wq, wk = w_row[:, 0:M], w_row[:, at_q:at_k], w_row[:, at_k:at_v]
        wv, wo = w_row[:, at_v:at_o], w_row[:, at_o:at_o + D]
        w_chan = sb("w_chan", [P, 3 * INNER + 2 + D], F32)
        bin_c, w1_c, b1_c = w_chan[:, 0:1], w_chan[:, 1:1 + INNER], w_chan[:, 1 + INNER:1 + 2 * INNER]
        w2_c = w_chan[:, 1 + 2 * INNER:1 + 3 * INNER]
        b2_c, wout = w_chan[:, 1 + 3 * INNER:2 + 3 * INNER], w_chan[:, 2 + 3 * INNER:]
        kshift = sb("kshift", [2 * G * HD, 1], F32)
        bout = sb("bout", [P, D], F32)
        minus_half = sb("minus_half", [P, NT], F32)
        zeros = sb("zeros", [2 * SETS, P], F32)
        e_mask = sb("e_mask", [P, 3], F32)
        e_rows = sb("e_rows", [P, QEW], BF16)

        bias = sb("bias", [P, SETS, 2, QT, WIN], F32)
        q_set = sb("q_set", [P, SETS, 2, T], BF16)
        k_set = sb("k_set", [P, SETS, 2, T], BF16)
        v_set = sb("v_set", [P, SETS, QT, 32], F32)
        qe_stage = sb("qe_stage", [P, 2, QT, QEW], F32)
        q_last = sb("q_last", [P, 2, QT], F32)
        probs = sb("probs", [P, 8, BANK], F32)
        score_copy = sb("score_copy", [P, 2, WIN], BF16)
        near_max = sb("near_max", [P, 2, 2 * QT], F32)
        far_max = sb("far_max", [P, 2, 2 * QT], F32)
        row_max = sb("row_max", [P, 2 * QT], F32)
        neg_max = sb("neg_max", [2 * QT, 3, P], F32)
        neg_part = sb("neg_part", [2 * QT, 3, P], BF16)
        o_raw = sb("o_raw", [P, BANK], F32)
        o_recip = sb("o_recip", [P, 4, 4], F32)

        room = bias[:].rearrange("p s h t w -> p (s h t w)")
        used = [0]

        def part(cols, dt=F32):
            words = cols if dt == F32 else cols // 2
            v = room[:, used[0]:used[0] + words]
            used[0] += words
            return v if dt == F32 else v.bitcast(dt)

        w2_diag = part(PE_UNITS * P).rearrange("p (j n) -> p j n", j=PE_UNITS)
        x_in = part(NT * D).rearrange("p (t d) -> p t d", t=NT)
        xn = part(NT * D).rearrange("p (t d) -> p t d", t=NT)
        xn_t = part(NT * D)
        x_biased = part(NT * D).rearrange("p (t d) -> p t d", t=NT)
        s_t = part(T)
        hidden = part(4 * T).rearrange("p (j t) -> p j t", j=4)
        stats = part(NT * 6).rearrange("p (t s) -> p t s", t=NT)
        mean_var = part(NT * 2).rearrange("p (t s) -> p t s", t=NT)
        var_eps = part(NT)
        rstd = part(NT)
        hidden_flat = hidden.rearrange("p j t -> p (j t)")
        q_rest = part(NT * D)
        k_rest = hidden_flat[0:2 * G * HD, 0:NT * D]
        q32 = hidden_flat[:, NT * D:2 * NT * D]
        k32 = x_biased.rearrange("p t d -> p (t d)")[0:2 * G * HD, :]
        q_split = part(3 * NT * D, BF16).rearrange("p (s t) -> p s t", s=3)
        k_split_full = part(3 * NT * D, BF16)
        k_split = k_split_full[0:2 * G * HD, :].rearrange("p (s t) -> p s t", s=3)
        q_split_words = q_split.rearrange("p s t -> p (s t)").bitcast(F32)
        hidden_dve = q_split_words[:, 0:2 * T].rearrange("p (j t) -> p j t", j=2)
        hidden_own = q_split_words[:, 2 * T:3 * T]
        k_split_words = k_split_full.bitcast(F32)
        h_pre, g_sum, g_t = (k_split_words[:, T * i:T * i + T] for i in range(3))
        e_rev, e_rel, e_rest, e_low = part(QEW), part(QEW), part(QEW), part(QEW)
        e_part = part(3 * QEW, BF16).rearrange("p (s w) -> p s w", s=3)
        assert used[0] <= SETS * 2 * QT * WIN

        x_loaded = [sem(f"x_loaded{c}") for c in range(2)]
        rows_loaded = sem("rows_loaded")
        channels_loaded = sem("channels_loaded")
        e_loaded = sem("e_loaded")
        bout_loaded = sem("bout_loaded")
        ident_zero = sem("ident_zero")
        ident_ready = sem("ident_ready")
        consts_ready = sem("consts_ready")
        q_cleared = sem("q_cleared")
        k_ones = sem("k_ones")
        diag_ready = sem("diag_ready")
        bout_halved = sem("bout_halved")
        e_step = sem("e_step")
        e_ready = sem("e_ready")
        pads_written = sem("pads_written")
        stats_ready = sem("stats_ready")
        mean_ready = sem("mean_ready")
        var_ready = sem("var_ready")
        rstd_ready = sem("rstd_ready")
        xn_ready = sem("xn_ready")
        xnt_in_psum = sem("xnt_in_psum")
        xnt_by_act = sem("xnt_by_act")
        xnt_by_dve = sem("xnt_by_dve")
        x_biased_ready = sem("x_biased_ready")
        s_in_psum = sem("s_in_psum")
        s_by_act = sem("s_by_act")
        s_by_dve = sem("s_by_dve")
        h_by_act = sem("h_by_act")
        h_used = sem("h_used")
        h_for_dve = sem("h_for_dve")
        own_step = sem("own_step")
        g_step = sem("g_step")
        g_ready = sem("g_ready")
        y_in_psum = sem("y_in_psum")
        x_new = sem("x_new")
        q_in_psum = sem("q_in_psum")
        k_in_psum = sem("k_in_psum")
        v_in_psum = sem("v_in_psum")
        q_scaled = sem("q_scaled")
        k_shifted = sem("k_shifted")
        q_split_step = sem("q_split_step")
        k_split_step = sem("k_split_step")
        v_cleared = sem("v_cleared")
        v_ready = sem("v_ready")
        q_stored = sem("q_stored")
        k_stored = sem("k_stored")
        q_loaded = [sem(f"q_loaded{s}") for s in range(SETS)]
        kv_loaded = [sem(f"kv_loaded{s}") for s in range(SETS)]
        qe_in_psum = sem("qe_in_psum")
        qe_staged = sem("qe_staged")
        qe_stored = [sem(f"qe_stored{h}") for h in range(2)]
        bias_loaded = [sem(f"bias_loaded{h}") for h in range(2)]
        q_last_ready = sem("q_last_ready")
        bias_fixing = sem("bias_fixing")
        bias_ready = sem("bias_ready")
        scores_ready = sem("scores_ready")
        near_done = sem("near_done")
        far_done = sem("far_done")
        row_max_ready = sem("row_max_ready")
        max_in_psum = sem("max_in_psum")
        max_step = sem("max_step")
        max_rows_placed = sem("max_rows_placed")
        st_ready = sem("st_ready")
        exp_done = sem("exp_done")
        pv_done = sem("pv_done")
        o_copied = sem("o_copied")
        o_in_psum = sem("o_in_psum")
        recip_ready = sem("recip_ready")
        attn_ready = sem("attn_ready")
        at_in_psum = sem("at_in_psum")
        at_by_act = sem("at_by_act")
        at_by_dve = sem("at_by_dve")
        proj_in_psum = sem("proj_in_psum")
        x2_ready = sem("x2_ready")
        out_stored = sem("out_stored")
        pool_passed = sem("pool_passed")
        sp_passed = sem("sp_passed")

        x_dram = x.rearrange("(t p) d -> p t d", p=P)
        out_dram = out.rearrange("(t p) d -> p t d", p=P)
        Q_LOADS, KV_LOADS = 6, 7

        block = ctx.enter_context(nc.Block())

        def near_tiles(qt):
            return [kt for kt in (qt - 1, qt, qt + 1) if 0 <= kt < QT]

        def qe_bank(n):
            return OUT_BANK if n is not None and n < Q_FIRST and n % 2 else MISC

        @block.sync
        def _(sp):
            for c in range(2):
                sp.dma_start(x_in[:, 8 * c:8 * c + 8, :], x_dram[:, 8 * c:8 * c + 8, :]).then_inc(x_loaded[c], 16)
            sp.wait_ge(consts_ready, 2)
            sp.dma_start(qe_dram[:, 0:P], zeros[:]).then_inc(pads_written, 16)
            sp.dma_start(qe_dram[:, SLOT - P:SLOT], zeros[:]).then_inc(pads_written, 16)
            sp.wait_ge(q_cleared, 1)
            sp.dma_start(q_parts[:, 3 * HD:QD, :].rearrange("u r t -> u (r t)"),
                         q_set[0:2 * UNITS, :, :, :].rearrange("p s h t -> p (s h t)")[:, 0:3 * T]
                         ).then_inc(pads_written, 16)

            def store_q(b):
                sp.wait_ge(q_split_step, 5 * b + 5)
                for i in range(3):
                    dst = q_parts[b * H:(b + 1) * H, HD * i:HD * i + HD, :]
                    sp.dma_start(dst, q_split[:, i, b * T:(b + 1) * T]).then_inc(q_stored, 16)

            def store_k(b):
                sp.wait_ge(k_split_step, 5 * b + 5)
                for i in range(3):
                    dst = k_parts[b, :, HD * i:HD * i + HD, :]
                    sp.dma_start(dst, k_split[:, i, b * T:(b + 1) * T]).then_inc(k_stored, 16)

            def load_q(u, s):
                wait(sp, pv_done, QT * (u - SETS) + QT)
                hold(sp, sp_passed)
                for h in range(2):
                    for i, r in enumerate((0, 3, 5)):
                        times = Q_PART.count(i)
                        end = QD if i == 2 else HD * i + HD
                        src = one(q_parts.rearrange("(u h) r t -> u h r t", h=2)[:, h, HD * i:end, :], u)
                        rows = HB * h + HD * r
                        if times > 1:
                            src = src.rearrange("(o d) t -> o d t", o=1).broadcast_to([times, HD, T])
                        sp.dma_start(q_set[rows:rows + times * (end - HD * i), s, h, :], src).then_inc(q_loaded[s], 16)

            def load_kv(uk, s):
                for h in range(2):
                    for r, n in ((0, 3), (3, 2), (5, 1)):
                        b, g = (uk // G, uk % G)
                        if isinstance(uk, int):
                            src = k_parts[b].rearrange("(v g) r t -> g r v t", g=G)[g, 0:HD * n]
                        else:
                            src = k_parts[bass.ds(b, 1)].rearrange("o (v g) r t -> (o g) r v t", g=G)
                            src = src[bass.ds(g, 1), 0:HD * n].rearrange("o r v t -> (o r) v t")
                        rows = HB * h + HD * r
                        sp.dma_start(k_set[rows:rows + HD * n, s, :, :], src).then_inc(kv_loaded[s], 16)
                v_by_unit = v_all[:].rearrange("p b g k c -> p (b g) (k c)")
                src = v_by_unit[:, uk, :] if isinstance(uk, int) else v_by_unit[:, bass.ds(uk, 1), :]
                dst = v_set[:, s, :, :].rearrange("p k c -> p (k c)")
                if not isinstance(uk, int):
                    dst = v_set[:, s:s + 1, :, :].rearrange("p s k c -> p s (k c)")
                sp.dma_start(dst, src).then_inc(kv_loaded[s], 16)

            def one(ap, u):
                if isinstance(u, int):
                    return ap[u]
                v = ap[bass.ds(u, 1)]
                if len(v.shape) == 3:
                    return v.rearrange("o a b -> (o a) b")
                return v.rearrange("o a b c -> (o a) b c")

            def store_qe(u, s, h):
                sp.wait_ge(qe_staged, 8 * u + 4 * h + 4)
                hold(sp, sp_passed)
                wait(sp, bias_loaded[h], 16 * u)
                hold(sp, sp_passed)
                z = 2 * s + h
                dst = qe_dram[z, P:P + T * QEW].rearrange("(t p w) -> p t w", p=P, w=QEW)
                sp.dma_start(dst, qe_stage[:, h, :, :]).then_inc(qe_stored[h], 16)

            def load_skewed(u, s, h):
                sp.wait_ge(qe_stored[h], 16 * u + 16)
                hold(sp, sp_passed)
                wait(sp, st_ready, 4 * QT * (u - SETS + 1))
                hold(sp, sp_passed)
                z = 2 * s + h
                src = bass.AP(qe_dram.tensor, z * SLOT + P - 1, [[QEW - 1, P], [P * QEW, QT], [1, WIN]])
                sp.dma_start(bias[:, s, h, :, :], src).then_inc(bias_loaded[h], 16)

            def max_rows(u, s):
                sp.wait_ge(max_step, 5 * u + 5)
                hold(sp, sp_passed)
                for h in range(2):
                    for i in range(3):
                        row = HB * h + KS + i
                        sp.dma_start(q_set[row:row + 1, s, h, :],
                                     neg_part[QT * h:QT * h + QT, i, :]).then_inc(max_rows_placed, 16)

            def step(i, j, static, uk):
                if within(static, 3, UNITS):
                    load_q(i + 3, (j + 3) % SETS)
                    load_kv(uk, (j + 3) % SETS)
                if within(static, 2, UNITS):
                    store_qe(i + 2, (j + 2) % SETS, 1)
                    load_skewed(i + 2, (j + 2) % SETS, 1)
                if within(static, 1, UNITS):
                    max_rows(i + 1, (j + 1) % SETS)
                if within(static, 3, UNITS):
                    store_qe(i + 3, (j + 3) % SETS, 0)
                    load_skewed(i + 3, (j + 3) % SETS, 0)

            sp.wait_ge(k_ones, 1)
            store_q(0)
            sp.wait_ge(q_stored, 48)
            sp.wait_ge(pads_written, 48)
            load_q(0, 0)
            store_k(0)
            load_q(1, 1)
            store_qe(0, 0, 0)
            sp.wait_ge(k_stored, 48)
            sp.wait_ge(v_ready, NT)
            load_kv(0, 0)
            store_qe(0, 0, 1)
            load_skewed(0, 0, 0)
            load_skewed(0, 0, 1)
            store_qe(1, 1, 0)
            load_kv(0, 1)
            store_q(1)
            store_k(1)
            load_skewed(1, 1, 0)
            sp.wait_ge(q_stored, 96)
            sp.wait_ge(k_stored, 96)
            for i in range(-1, 1):
                step(i, i % SETS, i, (i + 3) // 2)
            with sp.Fori(0, LOOPS) as turn:
                for j in range(SETS):
                    step(turn * SETS + (1 + j), (1 + j) % SETS, None, turn * 2 + (2 + j // 2))
            for i in range(1 + LOOPS * SETS, UNITS):
                step(i, i % SETS, i, (i + 3) // 2)

            for c in range(4):
                sp.wait_ge(x_new, 4 + c + 1)
                sp.dma_start(out_dram[:, 4 * c:4 * c + 4, :], xn[:, 4 * c:4 * c + 4, :]).then_inc(out_stored, 16)
            sp.wait_ge(out_stored, 64)

        @block.gpsimd
        def _(pool):
            pool.memset(ident[:], 0.0).then_inc(ident_zero, 1)
            pool.wait_ge(ident_zero, 1)
            pool.affine_select(out=ident[:], in_=ident[:], compare_op=ALU.not_equal, fill=1.0, base=0,
                               pattern=[[-1, P]], channel_multiplier=1).then_inc(ident_ready, 1)
            pool.memset(minus_half[:], -0.5).then_inc(consts_ready, 1)
            pool.memset(zeros[:], 0.0).then_inc(consts_ready, 1)
            pool.wait_ge(consts_ready, 2)

            def rstd_of(f):
                for c in range(4):
                    cols = slice(4 * c, 4 * c + 4)
                    pool.wait_ge(var_ready, 4 * f + c + 1)
                    pool.tensor_tensor(rstd[:, cols], var_eps[:, cols], minus_half[:, cols], ALU.pow
                                       ).then_inc(rstd_ready, 1)

            def diagonals():
                for j in range(PE_UNITS):
                    pool.tensor_scalar(w2_diag[:, j, :], ident[:], w2_c[:, j:j + 1], None, ALU.mult).then_inc(diag_ready, 1)

            def x_biased_of(src):
                bout_all = bout[:].rearrange("p (o d) -> p o d", o=1).broadcast_to([P, NT, D])
                pool.tensor_tensor(x_biased, src, bout_all, ALU.add).then_inc(x_biased_ready, 1)

            rstd_of(0)
            pool.wait_ge(channels_loaded, 16)
            pool.wait_ge(ident_ready, 1)
            diagonals()
            pool.wait_ge(bout_loaded, 16)
            pool.tensor_scalar(bout[:], bout[:], 0.5, None, ALU.mult).then_inc(bout_halved, 1)
            pool.wait_ge(bout_halved, 1)
            x_biased_of(x_in)
            pool.memset(v_all[:], 0.0).then_inc(v_cleared, 1)
            pool.wait_ge(v_cleared, 1)
            pool.memset(v_all[:, :, :, :, HD:HD + 1], 1.0).then_inc(v_cleared, 1)
            pool.memset(k_set[:], 1.0).then_inc(k_ones, 1)
            rstd_of(1)

            def keep_last(u, h):
                pool.wait_ge(qe_staged, 8 * u + 4 * h + 4)
                wait(pool, bias_fixing, 2 * (2 * (u - 1) + h + 1))
                hold(pool, pool_passed)
                pool.tensor_copy(q_last[:, h, :], qe_stage[:, h, :, NE - 1:NE].rearrange("p t o -> p (t o)")
                                 ).then_inc(q_last_ready, 1)

            def fix(u, s, h):
                head = 2 * u + h
                left = bias[:, s, h, :, 0:P]
                right = bias[:, s, h, :, 2 * P:WIN]
                pool.wait_ge(bias_loaded[h], 16 * u + 16)
                hold(pool, pool_passed)
                pool.affine_select(out=left, in_=left, compare_op=ALU.is_ge, fill=0.0, base=-1,
                                   pattern=[[0, QT], [1, P]], channel_multiplier=-1).then_inc(bias_fixing, 1)
                pool.wait_ge(q_last_ready, head + 1)
                last = q_last[:, h, :].rearrange("p (t o) -> p t o", o=1).broadcast_to([P, QT, P])
                pool.tensor_tensor(right, right, last, ALU.subtract).then_inc(bias_fixing, 1)
                pool.wait_ge(bias_fixing, 2 * head + 2)
                hold(pool, pool_passed)
                pool.affine_select(out=right, in_=right, compare_op=ALU.is_ge, fill=0.0, base=-1,
                                   pattern=[[0, QT], [-1, P]], channel_multiplier=1).then_inc(bias_ready, 1)

            def step(i, j, static):
                if within(static, 2, UNITS):
                    keep_last(i + 2, 1)
                    fix(i + 2, (j + 2) % SETS, 1)
                if within(static, 3, UNITS):
                    keep_last(i + 3, 0)
                    fix(i + 3, (j + 3) % SETS, 0)

            for i in range(-3, 1):
                step(i, i % SETS, i)
            with pool.Fori(0, LOOPS) as turn:
                for j in range(SETS):
                    step(turn * SETS + (1 + j), (1 + j) % SETS, None)
            for i in range(1 + LOOPS * SETS, UNITS):
                step(i, i % SETS, i)

            pool.wait_ge(st_ready, 4 * QT * (UNITS - SETS + 1))
            diagonals()
            rstd_of(2)
            x_biased_of(x1[:])

        @block.scalar
        def _(act):
            def xn_t_copy(f):
                for c in (0, 2):
                    act.wait_ge(xnt_in_psum, 4 * f + c + 1)
                    act.copy(xn_t[:, c * BANK:(c + 1) * BANK], ps[:, c, :]).then_inc(xnt_by_act, 1)

            def ffn(f):
                act.wait_ge(s_in_psum, f + 1)
                act.activation(s_t[:, 0:BANK], ps[:, 4, :], ACT.Identity, bias=bin_c).then_inc(s_by_act, 1)
                act.wait_ge(s_by_act, f + 1)
                act.wait_ge(s_by_dve, f + 1)
                for j in ACT_ORDER:
                    if j < PE_UNITS:
                        if PE_UNITS * f + j >= 4:
                            act.wait_ge(h_used, PE_UNITS * f + j - 3)
                        dst, done = hidden[:, j % 4, :], h_by_act
                    else:
                        n = ACT_UNITS * f + j - PE_UNITS
                        if n >= 2:
                            act.wait_ge(g_step, 2 * (n - 1))
                        dst, done = hidden_dve[:, j % 2, :], h_for_dve
                    act.activation(dst, s_t, ACT.Relu, bias=b1_c[:, j:j + 1], scale=w1_c[:, j:j + 1]).then_inc(done, 1)

            act.dma_start(w_row[:], w_rows).then_inc(rows_loaded, 16)
            act.dma_start(w_chan[:], w_channels).then_inc(channels_loaded, 16)
            act.dma_start(bout[:], b_out.partition_broadcast(P)).then_inc(bout_loaded, 16)
            act.dma_start(e_rev[:, 0:NE], E_t).then_inc(e_loaded, 16)
            act.dma_start(e_mask[:], e_masks).then_inc(e_loaded, 16)
            act.dma_start(kshift[:], k_shift).then_inc(e_loaded, 16)
            act.wait_ge(channels_loaded, 16)
            xn_t_copy(0)
            ffn(0)
            xn_t_copy(1)
            act.wait_ge(e_loaded, 48)
            for b in range(B):
                for c in (2 * b, 2 * b + 1):
                    act.wait_ge(q_in_psum, c + 1)
                    act.mul(q32[:, c * BANK:(c + 1) * BANK], ps[:, c, :], (1.0 / HD) ** 0.5).then_inc(q_scaled, 1)
                for c in (2 * b, 2 * b + 1):
                    act.wait_ge(k_in_psum, c + 1)
                    act.activation(k32[:, c * BANK:(c + 1) * BANK], ps[0:2 * G * HD, 4 + c, :], ACT.Identity,
                                   bias=kshift[:, 0:1]).then_inc(k_shifted, 1)
            def stage_qe(at, bank):
                h, pair = key_tile(at) // 4, key_tile(at) % 4
                act.wait_ge(qe_in_psum, slot_no(at, 1, 1))
                wait(act, qe_stored[h], unit_no(at, 16))
                wait(act, q_last_ready, unit_no(at, 2, h - 1))
                act.copy(qe_stage[:, h, 2 * pair:2 * pair + 2, :].rearrange("p t w -> p (t w)"),
                         ps[:, bank, :]).then_inc(qe_staged, 1)

            def slot(at, static):
                for t in range(4):
                    if within(static, 0):
                        act.wait_ge(st_ready, slot_no(at, 4, t + 1))
                        if t == 0:
                            wait(act, pv_done, slot_no(at, 1, -1))
                        act.activation(probs[:, 4 * (at[1] % 2) + t, :], ps[:, T_BANK + t % 2, :],
                                       ACT.Exp).then_inc(exp_done, 1)
                    if t == 1 and within(static, Q_LEAD):
                        stage_qe(ahead(at, Q_LEAD), qe_bank(None if static is None else static + Q_LEAD))

            over_slots(act, slot)
            for c in (0, 2):
                act.wait_ge(at_in_psum, c + 1)
                act.copy(xn_t[:, c * BANK:(c + 1) * BANK], ps[:, c, :]).then_inc(at_by_act, 1)
            xn_t_copy(2)
            ffn(1)

        @block.vector
        def _(dve):
            dve.memset(o_recip[:], 1.0).then_inc(attn_ready, 2)
            dve.memset(q_set[:], 0.0).then_inc(q_cleared, 1)

            def layer_norm(f, src):
                arrived = x_loaded if f == 0 else (x_new if f == 1 else x2_ready)

                def statistics(c):
                    if f == 0 and c % 2 == 0:
                        dve.wait_ge(arrived[c // 2], 16)
                    if f > 0:
                        dve.wait_ge(arrived, c + 1)
                    for t in range(4 * c, 4 * c + 4):
                        dve.bn_stats(stats[:, t, :], src[:, t, :]).then_inc(stats_ready, 1)

                statistics(0)
                for c in range(4):
                    if c < 3:
                        statistics(c + 1)
                    for t in range(4 * c, 4 * c + 4):
                        dve.wait_ge(stats_ready, NT * f + t + 1)
                        dve.bn_aggr(mean_var[:, t, :], stats[:, t, :]).then_inc(mean_ready, 1)
                    dve.wait_ge(mean_ready, NT * f + 4 * c + 4)
                    dve.tensor_scalar(var_eps[:, 4 * c:4 * c + 4],
                                      mean_var[:, 4 * c:4 * c + 4, 1:2].rearrange("p t o -> p (t o)"), EPS, None,
                                      ALU.add).then_inc(var_ready, 1)
                for t in range(NT):
                    if t % 4 == 0:
                        dve.wait_ge(rstd_ready, 4 * f + t // 4 + 1)
                    dve.tensor_scalar(xn[:, t, :], src[:, t, :], mean_var[:, t, 0:1], rstd[:, t:t + 1],
                                      ALU.subtract, ALU.mult).then_inc(xn_ready, 1)
                for c in (1, 3):
                    dve.wait_ge(xnt_in_psum, 4 * f + c + 1)
                    dve.tensor_copy(xn_t[:, c * BANK:(c + 1) * BANK], ps[:, c, :]).then_inc(xnt_by_dve, 1)

            def ffn(f, dst):
                dve.wait_ge(s_in_psum, f + 1)
                dve.tensor_scalar(s_t[:, BANK:T], ps[:, 5, :], bin_c, None, ALU.add).then_inc(s_by_dve, 1)
                dve.wait_ge(s_by_act, f + 1)
                dve.wait_ge(s_by_dve, f + 1)
                for i in range(OWN_UNITS):
                    j, n = PE_UNITS + ACT_UNITS + i, OWN_UNITS * f + i
                    if n:
                        dve.wait_ge(own_step, 2 * n)
                    dve.tensor_scalar(h_pre, s_t, w1_c[:, j:j + 1], b1_c[:, j:j + 1], ALU.mult,
                                      ALU.add).then_inc(own_step, 1)
                    dve.wait_ge(own_step, 2 * n + 1)
                    if n:
                        dve.wait_ge(g_step, 2 * n)
                    dve.tensor_scalar(hidden_own, h_pre, 0.0, None, ALU.max).then_inc(own_step, 1)
                    dve.wait_ge(own_step, 2 * n + 2)
                    if i == 0:
                        dve.tensor_scalar(g_sum, hidden_own, w2_c[:, j:j + 1], None, ALU.mult).then_inc(g_step, 1)
                    else:
                        dve.scalar_tensor_tensor(out=g_sum, in0=hidden_own, scalar=w2_c[:, j:j + 1], in1=g_sum,
                                                 op0=ALU.mult, op1=ALU.add).then_inc(g_step, 1)
                    j = PE_UNITS + i
                    dve.wait_ge(h_for_dve, n + 1)
                    dve.wait_ge(g_step, 2 * n + 1)
                    dve.scalar_tensor_tensor(out=g_sum, in0=hidden_dve[:, j % 2, :], scalar=w2_c[:, j:j + 1], in1=g_sum,
                                             op0=ALU.mult, op1=ALU.add).then_inc(g_step, 1)
                dve.wait_ge(h_used, PE_UNITS * (f + 1))
                dve.wait_ge(g_step, 2 * OWN_UNITS * (f + 1))
                for c in range(2):
                    cols = slice(c * BANK, (c + 1) * BANK)
                    dve.scalar_tensor_tensor(out=g_t[:, cols], in0=ps[:, 6 + c, :], scalar=b2_c, in1=g_sum[:, cols],
                                             op0=ALU.add, op1=ALU.add).then_inc(g_ready, 1)
                dve.wait_ge(x_biased_ready, f + 1)
                for c in range(4):
                    dve.wait_ge(y_in_psum, 4 * f + c + 1)
                    dve.scalar_tensor_tensor(out=dst[:, 4 * c:4 * c + 4, :].rearrange("p t d -> p (t d)"),
                                             in0=ps[:, c, :], scalar=0.5,
                                             in1=x_biased[:, 4 * c:4 * c + 4, :].rearrange("p t d -> p (t d)"),
                                             op0=ALU.mult, op1=ALU.add).then_inc(x_new, 1)

            layer_norm(0, x_in)
            dve.wait_ge(channels_loaded, 16)
            ffn(0, x1)
            layer_norm(1, x1)
            dve.wait_ge(e_loaded, 48)
            dve.tensor_copy(e_rev[:, NE:QEW], e_rev[:, NE - 1:NE]).then_inc(e_step, 1)
            dve.wait_ge(e_step, 1)
            dve.tensor_scalar(e_rel, e_rev, e_rev[:, 0:1], None, ALU.subtract).then_inc(e_step, 1)
            dve.wait_ge(e_step, 2)
            dve.tensor_copy(e_part[:, 0, :], e_rel).then_inc(e_step, 1)
            dve.wait_ge(e_step, 3)
            dve.tensor_tensor(e_rest, e_rel, e_part[:, 0, :], ALU.subtract).then_inc(e_step, 1)
            dve.wait_ge(e_step, 4)
            dve.tensor_copy(e_part[:, 1, :], e_rest).then_inc(e_step, 1)
            dve.wait_ge(e_step, 5)
            dve.tensor_tensor(e_part[:, 2, :], e_rest, e_part[:, 1, :], ALU.subtract).then_inc(e_step, 1)
            dve.wait_ge(e_step, 6)
            dve.tensor_scalar(e_rows[:], e_part[:, 0, :], e_mask[:, 0:1], None, ALU.mult).then_inc(e_ready, 1)
            for i in (1, 2):
                dve.wait_ge(e_ready, i)
                dve.scalar_tensor_tensor(out=e_rows[:], in0=e_part[:, i, :], scalar=e_mask[:, i:i + 1], in1=e_rows[:],
                                         op0=ALU.mult, op1=ALU.add).then_inc(e_ready, 1)
            def split(parts, value, rest, b, step):
                cols = slice(b * T, (b + 1) * T)
                dve.tensor_copy(parts[:, 0, cols], value[:, cols]).then_inc(step, 1)
                dve.wait_ge(step, 5 * b + 1)
                dve.tensor_tensor(rest[:, cols], value[:, cols], parts[:, 0, cols], ALU.subtract).then_inc(step, 1)
                dve.wait_ge(step, 5 * b + 2)
                dve.tensor_copy(parts[:, 1, cols], rest[:, cols]).then_inc(step, 1)
                dve.wait_ge(step, 5 * b + 3)
                dve.tensor_tensor(value[:, cols], rest[:, cols], parts[:, 1, cols], ALU.subtract).then_inc(step, 1)
                dve.wait_ge(step, 5 * b + 4)
                dve.tensor_copy(parts[:, 2, cols], value[:, cols]).then_inc(step, 1)

            dve.wait_ge(q_scaled, 2)
            split(q_split, q32, q_rest, 0, q_split_step)
            dve.wait_ge(k_shifted, 2)
            split(k_split, k32, k_rest, 0, k_split_step)
            dve.wait_ge(v_in_psum, 1)
            dve.wait_ge(v_cleared, 2)
            for t in range(NT):
                dve.tensor_copy(v_all[:, t // QT, :, t % QT, 0:HD],
                                ps[:, MISC, 32 * t:32 * t + 32].rearrange("p (g d) -> p g d", g=G)
                                ).then_inc(v_ready, 1)

            dve.wait_ge(q_scaled, 4)
            split(q_split, q32, q_rest, 1, q_split_step)
            dve.wait_ge(k_shifted, 4)
            split(k_split, k32, k_rest, 1, k_split_step)

            def score_max(at, which):
                s, tile = set_of(at), 2 * key_tile(at) + which
                h, qt, par = tile // QT, tile % QT, s % 2
                near = len(near_tiles(qt)) * P
                first = (near_tiles(qt)[0] - qt + 1) * P
                base = S_BANK + 2 * which
                cols = ps[:, base:base + 2, :].rearrange("p b n -> p (b n)")
                if qt == 0:
                    dve.wait_ge(bias_ready, unit_no(at, 2, h + 1))
                dve.wait_ge(scores_ready, slot_no(at, 2, which + 1))
                wait(dve, near_done, slot_no(at, 2, which - 1))
                dve.tensor_reduce(far_max[:, par, tile:tile + 1], cols[:, near:2 * BANK], AX_X,
                                  ALU.max).then_inc(far_done, 1)
                dve.tensor_tensor_reduce(score_copy[:, tile % 2, 0:near],
                                         cols[:, 0:near],
                                         bias[:, s, h, qt, first:first + near], 1.0, -3.0e38, ALU.add, ALU.max,
                                         near_max[:, par, tile:tile + 1]).then_inc(near_done, 1)

            def unit_max(at):
                par = set_of(at) % 2
                dve.wait_ge(near_done, unit_no(at, 16, 16))
                dve.wait_ge(far_done, unit_no(at, 16, 16))
                dve.tensor_tensor(row_max[:], near_max[:, par, :], far_max[:, par, :], ALU.max).then_inc(row_max_ready, 1)

            def max_parts(at):
                dve.wait_ge(max_in_psum, unit_no(at, 1, 1))
                wait(dve, max_rows_placed, unit_no(at, 96))
                dve.tensor_scalar(neg_max[:, 0, :], ps[0:2 * QT, MISC, 0:P], -1.0, None, ALU.mult).then_inc(max_step, 1)
                dve.wait_ge(max_step, unit_no(at, 5, 1))
                dve.tensor_copy(neg_part[:, 0, :], neg_max[:, 0, :]).then_inc(max_step, 1)
                dve.wait_ge(max_step, unit_no(at, 5, 2))
                dve.tensor_tensor(neg_max[:, 1, :], neg_max[:, 0, :], neg_part[:, 0, :], ALU.subtract).then_inc(max_step, 1)
                dve.wait_ge(max_step, unit_no(at, 5, 3))
                dve.tensor_copy(neg_part[:, 1, :], neg_max[:, 1, :]).then_inc(max_step, 1)
                dve.wait_ge(max_step, unit_no(at, 5, 4))
                dve.tensor_tensor(neg_part[:, 2, :], neg_max[:, 1, :], neg_part[:, 1, :], ALU.subtract).then_inc(max_step, 1)

            def copy_out(at):
                dve.wait_ge(pv_done, unit_no(at, QT, QT))
                dve.wait_ge(attn_ready, unit_no(at, 2, 2))
                dve.tensor_copy(o_raw[:], ps[:, OUT_BANK, :]).then_inc(o_copied, 1)

            def normalise(at):
                dst = [attn[:, 4 * f:4 * f + 4, bass.ds(unit_no(at, 2 * HD), 2 * HD)]
                       .rearrange("p c (h d) -> p c h d", h=2) for f in range(2)]
                dve.wait_ge(o_in_psum, unit_no(at, 1, 1))
                o = ps[:, MISC, :].rearrange("p (c h f j) -> p c h f j", c=4, h=2, f=2)
                dve.reciprocal(o_recip[:].rearrange("p c (a o) -> p c a o", o=1),
                               ps[:, MISC, :].rearrange("p (c a j) -> p c a j", c=4, a=4)[:, :, :, HD:HD + 1]
                               ).then_inc(recip_ready, 1)
                r = o_recip[:].rearrange("p c (h f o) -> p c h f o", h=2, f=2)
                dve.wait_ge(recip_ready, unit_no(at, 1, 1))
                for f in range(2):
                    dve.tensor_tensor(dst[f], o[:, :, :, f, 0:HD], r[:, :, :, f, :].broadcast_to([P, 4, 2, HD]),
                                      ALU.mult).then_inc(attn_ready, 1)

            def slot(at, static):
                if static == -M_LEAD:
                    max_parts(ahead(at, M_LEAD))
                s_at = ahead(at, S_LEAD)
                if within(static, S_LEAD):
                    score_max(s_at, 0)
                if key_tile(at) == 0 and within(static, -QT):
                    copy_out(ahead(at, -QT))
                if key_tile(at) == QT - M_LEAD and within(static, M_LEAD) and static != -M_LEAD:
                    max_parts(ahead(at, M_LEAD))
                if key_tile(at) == 1 and within(static, -QT):
                    normalise(ahead(at, -QT))
                if within(static, S_LEAD):
                    score_max(s_at, 1)
                    if key_tile(s_at) == QT - 1:
                        unit_max(s_at)

            over_slots(dve, slot)

            for c in (1, 3):
                dve.wait_ge(at_in_psum, c + 1)
                dve.tensor_copy(xn_t[:, c * BANK:(c + 1) * BANK], ps[:, c, :]).then_inc(at_by_dve, 1)
            for c in range(4):
                dve.wait_ge(proj_in_psum, c + 1)
                cols = x1[:, 4 * c:4 * c + 4, :].rearrange("p t d -> p (t d)")
                dve.tensor_tensor(cols, ps[:, 4 + c, :], cols, ALU.add).then_inc(x2_ready, 1)
            layer_norm(2, x1[:])
            ffn(1, xn)

        @block.tensor
        def _(pe):
            def transposes(f):
                for c in range(4):
                    for t in range(4 * c, 4 * c + 4):
                        pe.wait_ge(xn_ready, NT * f + t + 1)
                        last = pe.transpose(ps[:, c, P * (t % 4):P * (t % 4) + P], xn[:, t, :], ident[:])
                    last.then_inc(xnt_in_psum, 1)
                pe.wait_ge(xnt_by_act, 2 * f + 2)
                pe.wait_ge(xnt_by_dve, 2 * f + 2)

            def ffn(f):
                for b in range(B):
                    for c in range(2):
                        cols = slice(b * T + c * BANK, b * T + (c + 1) * BANK)
                        last = pe.matmul(ps[M * b:M * b + M, 4 + c, :], win, xn_t[:, cols], start=True, stop=True)
                last.then_inc(s_in_psum, 1)
                pe.wait_ge(diag_ready, PE_UNITS * (f + 1))
                for j in range(PE_UNITS):
                    pe.wait_ge(h_by_act, PE_UNITS * f + j + 1)
                    for c in range(2):
                        last = pe.matmul(ps[:, 6 + c, :], w2_diag[:, j, :], hidden[:, j % 4, c * BANK:(c + 1) * BANK],
                                         start=(j == 0), stop=(j == PE_UNITS - 1))
                    last.then_inc(h_used, 1)
                pe.wait_ge(g_ready, 2 * f + 2)
                for t in range(NT):
                    rows = slice(M * (t // QT), M * (t // QT) + M)
                    last = pe.matmul(ps[:, t // 4, P * (t % 4):P * (t % 4) + P],
                                     g_t[rows, P * (t % QT):P * (t % QT) + P], wout[rows, :], start=True, stop=True)
                    if t % 4 == 3:
                        last.then_inc(y_in_psum, 1)

            pe.wait_ge(ident_ready, 1)
            transposes(0)
            pe.wait_ge(rows_loaded, 16)
            pe.wait_ge(channels_loaded, 16)
            ffn(0)
            pe.wait_ge(x_new, 4)
            transposes(1)
            for b in range(B):
                for c in (2 * b, 2 * b + 1):
                    cols = slice(c * BANK, (c + 1) * BANK)
                    pe.matmul(ps[:, c, :], wq, xn_t[:, cols], start=True, stop=True).then_inc(q_in_psum, 1)
                for c in (2 * b, 2 * b + 1):
                    cols = slice(c * BANK, (c + 1) * BANK)
                    pe.matmul(ps[0:2 * G * HD, 4 + c, :], wk, xn_t[:, cols], start=True, stop=True).then_inc(k_in_psum, 1)
            pe.wait_ge(q_scaled, 1)
            for t in range(NT):
                last = pe.matmul(ps[:, MISC, 32 * t:32 * t + 32], xn_t[:, P * t:P * t + P], wv, start=True, stop=True)
            last.then_inc(v_in_psum, 1)
            pe.wait_ge(q_scaled, 4)
            pe.wait_ge(k_shifted, 4)
            pe.wait_ge(v_ready, NT)
            pe.wait_ge(e_ready, 3)

            def qe(at, bank):
                s, h, pair = set_of(at), key_tile(at) // 4, key_tile(at) % 4
                if key_tile(at) == 0:
                    pe.wait_ge(q_loaded[s], loads_of(at, Q_LOADS))
                wait(pe, qe_staged, slot_no(at) if bank == MISC else slot_no(at, 1, -1))
                for i in range(2):
                    qt = 2 * pair + i
                    last = pe.matmul(ps[:, bank, QEW * i:QEW * i + QEW], q_set[:, s, h, P * qt:P * qt + P],
                                     e_rows[:], start=True, stop=True)
                last.then_inc(qe_in_psum, 1)

            def scores(at, which):
                s, tile = set_of(at), 2 * key_tile(at) + which
                h, qt = tile // QT, tile % QT
                near = near_tiles(qt)
                order = near + [kt for kt in range(QT) if kt not in near]
                wait(pe, near_done, slot_no(at, 2, which - 1))
                wait(pe, far_done, slot_no(at, 2, which - 1))
                i = 0
                while i < QT:
                    n = 1
                    while (i + n < QT and order[i + n] == order[i] + n and (i + n) % 4
                           and (order[i + n] > qt) == (order[i] > qt)):
                        n += 1
                    kt = order[i]
                    last = pe.matmul(ps[:, S_BANK + 2 * which + i // 4, P * (i % 4):P * (i % 4 + n)],
                                     q_set[:, s, h, P * qt:P * qt + P],
                                     k_set[:, s, int(kt > qt), P * kt:P * (kt + n)], start=True, stop=True)
                    i += n
                last.then_inc(scores_ready, 1)

            def exponents(at, t):
                s, kt = set_of(at), key_tile(at)
                h, half = t // 2, t % 2
                bank = T_BANK + t % 2
                wait(pe, exp_done, slot_no(at, 4, t - 1))
                first = True
                for i in range(4):
                    qt = 4 * half + i
                    if abs(qt - kt) <= 1:
                        w = (kt - qt + 1) * P
                        pe.matmul(ps[:, bank, P * i:P * i + P], bias[:, s, h, qt, w:w + P], ident[:],
                                  is_transpose=True, start=first, stop=False, skip_group_check=True)
                        first = False
                cut = min(max(kt - 4 * half, 0), 4)
                for var, a, b in ((1, 0, cut), (0, cut, 4)):
                    if a < b:
                        last = pe.matmul(ps[:, bank, P * a:P * b], k_set[:, s, var, P * kt:P * kt + P],
                                         q_set[:, s, h, P * (4 * half + a):P * (4 * half + b)],
                                         start=first, stop=True, skip_group_check=True)
                        first = False
                last.then_inc(st_ready, 1)

            def weigh(at):
                s, kt = set_of(at), key_tile(at)
                if kt == 0:
                    wait(pe, o_copied, unit_no(at))
                pe.wait_ge(exp_done, slot_no(at, 4, 4))
                for t in range(4):
                    last = pe.matmul(ps[32 * t:32 * t + 32, OUT_BANK, :], v_set[:, s, kt, :],
                                     probs[:, 4 * (at[1] % 2) + t, :], start=(kt == 0), stop=(kt == QT - 1))
                last.then_inc(pv_done, 1)

            def max_to_rows(at):
                pe.wait_ge(row_max_ready, unit_no(at, 1, 1))
                pe.transpose(ps[0:2 * QT, MISC, 0:P], row_max[:], ident[:]).then_inc(max_in_psum, 1)

            def outputs_to_rows(at):
                pe.wait_ge(o_copied, unit_no(at, 1, 1))
                for c in range(4):
                    last = pe.transpose(ps[:, MISC, P * c:P * c + P], o_raw[:, P * c:P * c + P], ident[:])
                last.then_inc(o_in_psum, 1)

            def misc_free(at, static, of_slot):
                if of_slot and within(static, Q_LEAD):
                    pe.wait_ge(qe_staged, slot_no(at, 1, Q_LEAD + 1))
                elif within(static, Q_LEAD - 1):
                    pe.wait_ge(qe_staged, slot_no(at, 1, Q_LEAD))

            def slot(at, static):
                kt = key_tile(at)
                s_at = ahead(at, S_LEAD)
                if within(static, 0):
                    if kt == 0:
                        pe.wait_ge(max_rows_placed, unit_no(at, 96, 96))
                        pe.wait_ge(bias_ready, unit_no(at, 2, 2))
                    exponents(at, 0)
                    exponents(at, 1)
                if static == -M_LEAD:
                    misc_free(at, static, False)
                    max_to_rows(ahead(at, M_LEAD))
                if within(static, S_LEAD):
                    if key_tile(s_at) == 0:
                        pe.wait_ge(kv_loaded[set_of(s_at)], loads_of(s_at, KV_LOADS))
                    scores(s_at, 0)
                if within(static, Q_LEAD) and (static is None or static + Q_LEAD >= Q_FIRST):
                    if (kt == QT - M_LEAD + 1 and within(static, M_LEAD)) or static == -M_LEAD:
                        pe.wait_ge(max_step, unit_no(ahead(at, M_LEAD), 5, 1))
                    if kt == 2 and within(static, -QT):
                        pe.wait_ge(attn_ready, unit_no(ahead(at, -QT), 2, 4))
                    qe(ahead(at, Q_LEAD), MISC)
                if within(static, 0):
                    exponents(at, 2)
                if within(static, -1):
                    weigh(ahead(at, -1))
                if kt == QT - M_LEAD and within(static, M_LEAD) and static != -M_LEAD:
                    misc_free(at, static, True)
                    max_to_rows(ahead(at, M_LEAD))
                if kt == 1 and within(static, -QT):
                    misc_free(at, static, True)
                    outputs_to_rows(ahead(at, -QT))
                if within(static, 0):
                    exponents(at, 3)
                if within(static, S_LEAD):
                    scores(s_at, 1)

            for n in range(Q_FIRST):
                qe((0, n), qe_bank(n))
            over_slots(pe, slot)

            pe.wait_ge(attn_ready, 2 * UNITS + 2)
            for c in range(4):
                for t in range(4 * c, 4 * c + 4):
                    b, qt = t // QT, t % QT
                    last = pe.transpose(ps[:, c, P * (t % 4):P * (t % 4) + P],
                                        attn[:, qt, b * D:b * D + D], ident[:])
                last.then_inc(at_in_psum, 1)
            pe.wait_ge(at_by_act, 2)
            pe.wait_ge(at_by_dve, 2)
            for t in range(NT):
                last = pe.matmul(ps[:, 4 + t // 4, P * (t % 4):P * (t % 4) + P], xn_t[:, P * t:P * t + P], wo,
                                 start=True, stop=True)
                if t % 4 == 3:
                    last.then_inc(proj_in_psum, 1)
            transposes(2)
            ffn(1)


def kernel(L0_attn_x, L0_attn_Wq, L0_attn_Wk, L0_attn_Wv, L0_attn_Wo, L0_attn_E, L0_ffn_Win, L0_ffn_bin_,
           L0_ffn_W1, L0_ffn_b1, L0_ffn_W2, L0_ffn_b2, L0_ffn_Wout, L0_ffn_bout):
    import numpy as np
    import concourse.bacc as bacc
    from concourse import mybir as my
    from concourse.bass_utils import run_bass_kernel_spmd

    E = np.asarray(L0_attn_E)
    win, wq, wk, wv, wo = (np.asarray(L0_ffn_Win), np.asarray(L0_attn_Wq).T, np.asarray(L0_attn_Wk).T,
                           np.asarray(L0_attn_Wv).T, np.asarray(L0_attn_Wo).T)
    channels = np.concatenate([np.asarray(L0_ffn_bin_)[:, None], L0_ffn_W1, L0_ffn_b1, L0_ffn_W2,
                               np.asarray(L0_ffn_b2)[:, None], L0_ffn_Wout], axis=1)
    masks = np.zeros((P, 3), np.float32)
    for base in (0, HB):
        for r, k in enumerate(K_PART):
            masks[base + HD * r:base + HD * r + HD, k] = 1.0
    arrays = {
        "x": np.asarray(L0_attn_x).reshape(B * T, D),
        "w_rows": np.concatenate([win, wq, wk, wk, wv, wo], axis=1),
        "w_channels": np.concatenate([channels, channels], axis=0),
        "E_t": np.tile(E[::-1].T, (P // HD, 1)),
        "e_masks": masks,
        "k_shift": np.concatenate([np.tile(E[NE - 1], G), np.tile(E[0], G)])[:, None],
        "b_out": L0_ffn_bout,
    }
    nc = bacc.Bacc("TRN2", target_bir_lowering=False, num_devices=1)
    feeds, args = {}, []
    for name, a in arrays.items():
        a = np.ascontiguousarray(a)
        feeds[f"in_{name}"] = a
        args.append(nc.dram_tensor(f"in_{name}", a.shape, my.dt.from_np(a.dtype), kind="ExternalInput").ap())
    args.append(nc.dram_tensor("out", [B * T, D], F32, kind="ExternalOutput").ap())
    macaron_attention(nc, *args)
    r = run_bass_kernel_spmd(nc, [feeds], core_ids=[0])
    return r.results[0]["out"].reshape(B, T, D)
```

```python
from contextlib import ExitStack

import concourse.bass as bass
from concourse import mybir

F32 = mybir.dt.float32
BF16 = mybir.dt.bfloat16
ALU = mybir.AluOpType
ACT = mybir.ActivationFunctionType
AX_X = mybir.AxisListType.X

P = 128
B, T, D = 2, 1024, 128
H, G, HD = 16, 4, 8
REACH = 127
NE = 2 * REACH + 1
M, INNER = 64, 16
EPS = 1e-5
NT = B * T // P
QT = T // P
UNITS = B * H // 2
SETS = 4
BANK = 512
WIN = 3 * P
QEW = 256
SLOT = P + T * QEW + P

Q_PART = (0, 0, 0, 1, 1, 2)
K_PART = (0, 1, 2, 0, 1, 0)
KS = HD * len(Q_PART)
KM = KS + 3
QD = 3 * HD + 3
HB = 64

PE_UNITS, ACT_UNITS = 10, 4
OWN_UNITS = INNER - PE_UNITS - ACT_UNITS
ACT_ORDER = (0, 10, 1, 2, 11, 3, 4, 12, 5, 6, 13, 7, 8, 9)
assert sorted(ACT_ORDER) == list(range(PE_UNITS + ACT_UNITS))
ACT_FIRST = 11
PE_FIRST = sum(j < PE_UNITS for j in ACT_ORDER[:ACT_FIRST])
DVE_UNITS = OWN_UNITS + ACT_UNITS
DVE_ORDER = (14, 10, 11, 15, 12, 13)

S_LEAD = 12
M_LEAD = S_LEAD - 8
Q_LEAD = 20
Q_FIRST = 2 * QT
SLOTS = UNITS * QT
BODY = SETS * QT
LOOP_FROM = QT
LOOPS = (SLOTS - Q_LEAD - LOOP_FROM) // BODY
LOOP_TO = LOOP_FROM + LOOPS * BODY


def wait(eng, sem, value):
    if isinstance(value, int) and value <= 0:
        return
    eng.wait_ge(sem, value)


def hold(eng, passed):
    eng.sem_inc(passed, 1)


def over_slots(eng, slot):
    for n in range(-Q_LEAD, LOOP_FROM):
        slot((0, n), n)
    with eng.Fori(0, LOOPS) as turn:
        for j in range(LOOP_FROM, LOOP_FROM + BODY):
            slot((turn, j), None)
    for n in range(LOOP_TO, SLOTS + 2):
        slot((0, n), n)


def ahead(at, lead):
    return at[0], at[1] + lead


def slot_no(at, times=1, plus=0):
    return at[0] * (BODY * times) + (at[1] * times + plus)


def unit_no(at, times=1, plus=0):
    return at[0] * (SETS * times) + (at[1] // QT * times + plus)


def key_tile(at):
    return at[1] % QT


def set_of(at):
    return at[1] // QT % SETS


def loads_of(at, loads):
    return at[0] * (16 * loads) + 16 * loads * (at[1] // BODY + 1)


def within(static, lead, count=SLOTS):
    return static is None or 0 <= static + lead < count


def macaron_attention(nc, x, w_rows, w_channels, E_t, e_masks, k_shift, b_out, out):
    with ExitStack() as ctx:
        def sb(name, shape, dt):
            return ctx.enter_context(nc.sbuf_tensor(name, shape, dt))

        def sem(name):
            return ctx.enter_context(nc.semaphore(name))

        q_parts = nc.dram_tensor("q_parts", [2 * UNITS, QD, T], BF16, kind="Internal").ap()
        k_parts = nc.dram_tensor("k_parts", [B, 2 * G, 3 * HD, T], BF16, kind="Internal").ap()
        qe_dram = nc.dram_tensor("qe_dram", [SETS * 2, SLOT], F32, kind="Internal").ap()

        ps = ctx.enter_context(nc.psum_tensor("ps", [P, 8, BANK], F32))
        MISC, OUT_BANK, T_BANK, S_BANK = 0, 1, 2, 4

        ident = sb("ident", [P, P], F32)
        x1 = sb("x1", [P, NT, D], F32)
        attn = sb("attn", [P, QT, B * D], F32)
        v_all = sb("v_all", [P, B, G, QT, 32], F32)
        w_row = sb("w_row", [P, M + D + 3 * G * HD + D], F32)
        at_q, at_k, at_v, at_o = M, M + D, M + D + 2 * G * HD, M + D + 3 * G * HD
        win, wq, wk = w_row[:, 0:M], w_row[:, at_q:at_k], w_row[:, at_k:at_v]
        wv, wo = w_row[:, at_v:at_o], w_row[:, at_o:at_o + D]
        w_chan = sb("w_chan", [P, 3 * INNER + 2 + D], F32)
        bin_c, w1_c, b1_c = w_chan[:, 0:1], w_chan[:, 1:1 + INNER], w_chan[:, 1 + INNER:1 + 2 * INNER]
        w2_c = w_chan[:, 1 + 2 * INNER:1 + 3 * INNER]
        b2_c, wout = w_chan[:, 1 + 3 * INNER:2 + 3 * INNER], w_chan[:, 2 + 3 * INNER:]
        kshift = sb("kshift", [2 * G * HD, 1], F32)
        bout = sb("bout", [P, D], F32)
        minus_half = sb("minus_half", [P, NT], F32)
        zeros = sb("zeros", [2 * SETS, P], F32)
        e_mask = sb("e_mask", [P, 3], F32)
        e_rows = sb("e_rows", [P, QEW], BF16)

        bias = sb("bias", [P, SETS, 2, QT, WIN], F32)
        q_set = sb("q_set", [P, SETS, 2, T], BF16)
        k_set = sb("k_set", [P, SETS, 2, T], BF16)
        v_set = sb("v_set", [P, SETS, QT, 32], F32)
        qe_stage = sb("qe_stage", [P, 2, QT, QEW], F32)
        q_last = sb("q_last", [P, 2, QT], F32)
        probs = sb("probs", [P, 8, BANK], F32)
        score_copy = sb("score_copy", [P, 2, WIN], BF16)
        near_max = sb("near_max", [P, 2, 2 * QT], F32)
        far_max = sb("far_max", [P, 2, 2 * QT], F32)
        row_max = sb("row_max", [P, 2 * QT], F32)
        neg_max = sb("neg_max", [2 * QT, 3, P], F32)
        neg_part = sb("neg_part", [2 * QT, 3, P], BF16)
        o_raw = sb("o_raw", [P, BANK], F32)
        o_recip = sb("o_recip", [P, 4, 4], F32)

        room = bias[:].rearrange("p s h t w -> p (s h t w)")
        used = [0]

        def part(cols, dt=F32):
            words = cols if dt == F32 else cols // 2
            v = room[:, used[0]:used[0] + words]
            used[0] += words
            return v if dt == F32 else v.bitcast(dt)

        def tiles(cols=QT * D):
            return part(cols).rearrange("p (t d) -> p t d", d=D)

        w2_diag = part(PE_UNITS * P).rearrange("p (j n) -> p j n", j=PE_UNITS)
        x_in, xn, xn_t, x_biased = [tiles()], [tiles()], [part(T)], [tiles()]
        hidden = part(4 * BANK).rearrange("p (j t) -> p j t", j=4)
        s_t = part(T).rearrange("p (b t) -> p b t", b=B)
        hidden_dve = part(ACT_UNITS * BANK).rearrange("p (j t) -> p j t", j=ACT_UNITS)
        hidden_own, h_pre = part(BANK), part(BANK)
        g_sum = part(T).rearrange("p (b t) -> p b t", b=B)
        g_t = part(T).rearrange("p (b t) -> p b t", b=B)
        stats = part(NT * 6).rearrange("p (t s) -> p t s", t=NT)
        mean_var = part(NT * 2).rearrange("p (t s) -> p t s", t=NT)
        var_eps = part(NT)
        rstd = part(NT)
        e_rev = part(QEW)
        q_split, k_split = [], []
        for b in range(B):
            if b == 1:
                for room_of_b in (x_in, xn, x_biased):
                    room_of_b.append(tiles())
                xn_t.append(part(T))
            q_split.append(part(3 * T, BF16).rearrange("p (s t) -> p s t", s=3))
            k_split.append(part(3 * T, BF16)[0:2 * G * HD, :].rearrange("p (s t) -> p s t", s=3))
        e_room = q_split[1].rearrange("p s t -> p (s t)").bitcast(F32)
        e_rel, e_rest = e_room[:, 0:QEW], e_room[:, QEW:2 * QEW]
        e_part = e_room[:, 2 * QEW:4 * QEW].bitcast(BF16)[:, 0:3 * QEW].rearrange("p (s w) -> p s w", s=3)
        q32 = [v.rearrange("p t d -> p (t d)") for v in xn]
        q_rest = [v.rearrange("p t d -> p (t d)") for v in x_in]
        k32 = [v.rearrange("p t d -> p (t d)")[0:2 * G * HD, :] for v in x_biased]
        k_rest = [v[0:2 * G * HD, :] for v in xn_t]
        assert used[0] <= SETS * 2 * QT * WIN

        x_loaded = [sem(f"x_loaded{c}") for c in range(2)]
        rows_loaded = sem("rows_loaded")
        channels_loaded = sem("channels_loaded")
        e_loaded = sem("e_loaded")
        bout_loaded = sem("bout_loaded")
        ident_zero = sem("ident_zero")
        ident_ready = sem("ident_ready")
        consts_ready = sem("consts_ready")
        q_cleared = sem("q_cleared")
        k_ones = sem("k_ones")
        diag_ready = sem("diag_ready")
        bout_halved = sem("bout_halved")
        e_step = sem("e_step")
        e_ready = sem("e_ready")
        pads_written = sem("pads_written")
        stats_ready = sem("stats_ready")
        mean_ready = sem("mean_ready")
        var_ready = sem("var_ready")
        rstd_ready = sem("rstd_ready")
        xn_ready = sem("xn_ready")
        xnt_in_psum = sem("xnt_in_psum")
        xnt_by_act = sem("xnt_by_act")
        xnt_by_dve = sem("xnt_by_dve")
        x_biased_ready = sem("x_biased_ready")
        s_in_psum = sem("s_in_psum")
        s_by_act = sem("s_by_act")
        h_by_act = sem("h_by_act")
        h_used = sem("h_used")
        h_for_dve = sem("h_for_dve")
        own_step = sem("own_step")
        g_step = sem("g_step")
        g_ready = sem("g_ready")
        y_in_psum = sem("y_in_psum")
        x_new = sem("x_new")
        q_in_psum = sem("q_in_psum")
        k_in_psum = sem("k_in_psum")
        v_in_psum = sem("v_in_psum")
        q_scaled = sem("q_scaled")
        k_shifted = sem("k_shifted")
        q_split_step = sem("q_split_step")
        k_split_step = sem("k_split_step")
        q_cut_by_act = sem("q_cut_by_act")
        q_rest_by_pool = sem("q_rest_by_pool")
        k_cut_by_act = sem("k_cut_by_act")
        k_rest_by_pool = sem("k_rest_by_pool")
        v_cleared = sem("v_cleared")
        v_ready = sem("v_ready")
        q_stored = sem("q_stored")
        k_stored = sem("k_stored")
        q_loaded = [sem(f"q_loaded{s}") for s in range(SETS)]
        kv_loaded = [sem(f"kv_loaded{s}") for s in range(SETS)]
        qe_in_psum = sem("qe_in_psum")
        qe_staged = sem("qe_staged")
        qe_stored = [sem(f"qe_stored{h}") for h in range(2)]
        bias_loaded = [sem(f"bias_loaded{h}") for h in range(2)]
        q_last_ready = sem("q_last_ready")
        bias_fixing = sem("bias_fixing")
        bias_ready = sem("bias_ready")
        scores_ready = sem("scores_ready")
        near_done = sem("near_done")
        far_done = sem("far_done")
        row_max_ready = sem("row_max_ready")
        max_in_psum = sem("max_in_psum")
        max_step = sem("max_step")
        max_rows_placed = sem("max_rows_placed")
        st_ready = sem("st_ready")
        exp_done = sem("exp_done")
        pv_done = sem("pv_done")
        o_copied = sem("o_copied")
        o_in_psum = sem("o_in_psum")
        recip_ready = sem("recip_ready")
        attn_ready = sem("attn_ready")
        at_in_psum = sem("at_in_psum")
        at_by_act = sem("at_by_act")
        at_by_dve = sem("at_by_dve")
        proj_in_psum = sem("proj_in_psum")
        x2_ready = sem("x2_ready")
        out_stored = sem("out_stored")
        pool_passed = sem("pool_passed")
        sp_passed = sem("sp_passed")

        x_dram = x.rearrange("(t p) d -> p t d", p=P)
        out_dram = out.rearrange("(t p) d -> p t d", p=P)
        Q_LOADS, KV_LOADS = 6, 7

        def bank(b, i):
            return 4 * b + i

        def flat(v):
            return v.rearrange("p t d -> p (t d)")

        block = ctx.enter_context(nc.Block())

        def near_tiles(qt):
            return [kt for kt in (qt - 1, qt, qt + 1) if 0 <= kt < QT]

        def bank_of_qe(n):
            return OUT_BANK if n is not None and n < Q_FIRST and n % 2 else MISC

        @block.sync
        def _(sp):
            for c in range(2):
                sp.dma_start(x_in[c], x_dram[:, 8 * c:8 * c + 8, :]).then_inc(x_loaded[c], 16)
            sp.wait_ge(consts_ready, 2)
            sp.dma_start(qe_dram[:, 0:P], zeros[:]).then_inc(pads_written, 16)
            sp.dma_start(qe_dram[:, SLOT - P:SLOT], zeros[:]).then_inc(pads_written, 16)
            sp.wait_ge(q_cleared, 1)
            sp.dma_start(q_parts[:, 3 * HD:QD, :].rearrange("u r t -> u (r t)"),
                         q_set[0:2 * UNITS, :, :, :].rearrange("p s h t -> p (s h t)")[:, 0:3 * T]
                         ).then_inc(pads_written, 16)

            def store_q(b):
                if b == 0:
                    sp.wait_ge(q_split_step, 5)
                else:
                    sp.wait_ge(q_cut_by_act, 3)
                for i in range(3):
                    dst = q_parts[b * H:(b + 1) * H, HD * i:HD * i + HD, :]
                    sp.dma_start(dst, q_split[b][:, i, :]).then_inc(q_stored, 16)

            def store_k(b):
                if b == 0:
                    sp.wait_ge(k_split_step, 5)
                else:
                    sp.wait_ge(k_cut_by_act, 3)
                for i in range(3):
                    dst = k_parts[b, :, HD * i:HD * i + HD, :]
                    sp.dma_start(dst, k_split[b][:, i, :]).then_inc(k_stored, 16)

            def load_q(u, s):
                wait(sp, pv_done, QT * (u - SETS) + QT)
                hold(sp, sp_passed)
                for h in range(2):
                    for i, r in enumerate((0, 3, 5)):
                        times = Q_PART.count(i)
                        end = QD if i == 2 else HD * i + HD
                        src = one(q_parts.rearrange("(u h) r t -> u h r t", h=2)[:, h, HD * i:end, :], u)
                        rows = HB * h + HD * r
                        if times > 1:
                            src = src.rearrange("(o d) t -> o d t", o=1).broadcast_to([times, HD, T])
                        sp.dma_start(q_set[rows:rows + times * (end - HD * i), s, h, :], src).then_inc(q_loaded[s], 16)

            def load_kv(uk, s):
                for h in range(2):
                    for r, n in ((0, 3), (3, 2), (5, 1)):
                        b, g = (uk // G, uk % G)
                        if isinstance(uk, int):
                            src = k_parts[b].rearrange("(v g) r t -> g r v t", g=G)[g, 0:HD * n]
                        else:
                            src = k_parts[bass.ds(b, 1)].rearrange("o (v g) r t -> (o g) r v t", g=G)
                            src = src[bass.ds(g, 1), 0:HD * n].rearrange("o r v t -> (o r) v t")
                        rows = HB * h + HD * r
                        sp.dma_start(k_set[rows:rows + HD * n, s, :, :], src).then_inc(kv_loaded[s], 16)
                v_by_unit = v_all[:].rearrange("p b g k c -> p (b g) (k c)")
                src = v_by_unit[:, uk, :] if isinstance(uk, int) else v_by_unit[:, bass.ds(uk, 1), :]
                dst = v_set[:, s, :, :].rearrange("p k c -> p (k c)")
                if not isinstance(uk, int):
                    dst = v_set[:, s:s + 1, :, :].rearrange("p s k c -> p s (k c)")
                sp.dma_start(dst, src).then_inc(kv_loaded[s], 16)

            def one(ap, u):
                if isinstance(u, int):
                    return ap[u]
                v = ap[bass.ds(u, 1)]
                if len(v.shape) == 3:
                    return v.rearrange("o a b -> (o a) b")
                return v.rearrange("o a b c -> (o a) b c")

            def store_qe(u, s, h):
                sp.wait_ge(qe_staged, 8 * u + 4 * h + 4)
                hold(sp, sp_passed)
                wait(sp, bias_loaded[h], 16 * u)
                hold(sp, sp_passed)
                z = 2 * s + h
                dst = qe_dram[z, P:P + T * QEW].rearrange("(t p w) -> p t w", p=P, w=QEW)
                sp.dma_start(dst, qe_stage[:, h, :, :]).then_inc(qe_stored[h], 16)

            def load_skewed(u, s, h):
                sp.wait_ge(qe_stored[h], 16 * u + 16)
                hold(sp, sp_passed)
                wait(sp, st_ready, 4 * QT * (u - SETS + 1))
                hold(sp, sp_passed)
                z = 2 * s + h
                src = bass.AP(qe_dram.tensor, z * SLOT + P - 1, [[QEW - 1, P], [P * QEW, QT], [1, WIN]])
                sp.dma_start(bias[:, s, h, :, :], src).then_inc(bias_loaded[h], 16)

            def max_rows(u, s):
                sp.wait_ge(max_step, 5 * u + 5)
                hold(sp, sp_passed)
                for h in range(2):
                    for i in range(3):
                        row = HB * h + KS + i
                        sp.dma_start(q_set[row:row + 1, s, h, :],
                                     neg_part[QT * h:QT * h + QT, i, :]).then_inc(max_rows_placed, 16)

            def step(i, j, static, uk):
                if within(static, 3, UNITS):
                    load_q(i + 3, (j + 3) % SETS)
                    load_kv(uk, (j + 3) % SETS)
                if within(static, 2, UNITS):
                    store_qe(i + 2, (j + 2) % SETS, 1)
                    load_skewed(i + 2, (j + 2) % SETS, 1)
                if within(static, 1, UNITS):
                    max_rows(i + 1, (j + 1) % SETS)
                if within(static, 3, UNITS):
                    store_qe(i + 3, (j + 3) % SETS, 0)
                    load_skewed(i + 3, (j + 3) % SETS, 0)

            sp.wait_ge(k_ones, 1)
            store_q(0)
            sp.wait_ge(q_stored, 48)
            sp.wait_ge(pads_written, 48)
            load_q(0, 0)
            store_k(0)
            store_qe(0, 0, 0)
            load_q(1, 1)
            store_qe(0, 0, 1)
            load_skewed(0, 0, 0)
            sp.wait_ge(k_stored, 48)
            sp.wait_ge(v_ready, QT)
            load_kv(0, 0)
            load_skewed(0, 0, 1)
            load_kv(0, 1)
            for h in range(2):
                store_qe(1, 1, h)
                load_skewed(1, 1, h)
            load_q(2, 2)
            load_kv(1, 2)
            store_q(1)
            store_k(1)
            max_rows(0, 0)
            store_qe(2, 2, 0)
            sp.wait_ge(q_stored, 96)
            sp.wait_ge(k_stored, 96)
            sp.wait_ge(v_ready, NT)
            load_skewed(2, 2, 0)
            step(0, 0, 0, 1)
            with sp.Fori(0, LOOPS) as turn:
                for j in range(SETS):
                    step(turn * SETS + (1 + j), (1 + j) % SETS, None, turn * 2 + (2 + j // 2))
            for i in range(1 + LOOPS * SETS, UNITS):
                step(i, i % SETS, i, (i + 3) // 2)

            for c in range(4):
                sp.wait_ge(x_new, 4 + c + 1)
                sp.dma_start(out_dram[:, 4 * c:4 * c + 4, :], xn[c // 2][:, 4 * (c % 2):4 * (c % 2) + 4, :]).then_inc(out_stored, 16)
            sp.wait_ge(out_stored, 64)

        @block.gpsimd
        def _(pool):
            pool.memset(ident[:], 0.0).then_inc(ident_zero, 1)
            pool.wait_ge(ident_zero, 1)
            pool.affine_select(out=ident[:], in_=ident[:], compare_op=ALU.not_equal, fill=1.0, base=0,
                               pattern=[[-1, P]], channel_multiplier=1).then_inc(ident_ready, 1)
            pool.memset(minus_half[:], -0.5).then_inc(consts_ready, 1)
            pool.memset(zeros[:], 0.0).then_inc(consts_ready, 1)
            pool.wait_ge(consts_ready, 2)

            def rstd_of(r):
                for c in range(2):
                    cols = slice(QT * (r % B) + 4 * c, QT * (r % B) + 4 * c + 4)
                    pool.wait_ge(var_ready, 2 * r + c + 1)
                    pool.tensor_tensor(rstd[:, cols], var_eps[:, cols], minus_half[:, cols], ALU.pow
                                       ).then_inc(rstd_ready, 1)

            def diagonals():
                for j in range(PE_UNITS):
                    pool.tensor_scalar(w2_diag[:, j, :], ident[:], w2_c[:, j:j + 1], None, ALU.mult).then_inc(diag_ready, 1)

            def x_biased_of(b, src):
                bout_all = bout[:].rearrange("p (o d) -> p o d", o=1).broadcast_to([P, QT, D])
                pool.tensor_tensor(x_biased[b], src, bout_all, ALU.add).then_inc(x_biased_ready, 1)

            rstd_of(0)
            rstd_of(1)
            pool.wait_ge(channels_loaded, 16)
            pool.wait_ge(ident_ready, 1)
            diagonals()
            pool.wait_ge(bout_loaded, 16)
            pool.tensor_scalar(bout[:], bout[:], 0.5, None, ALU.mult).then_inc(bout_halved, 1)
            pool.wait_ge(bout_halved, 1)
            for b in range(B):
                x_biased_of(b, x_in[b])
            pool.memset(v_all[:], 0.0).then_inc(v_cleared, 1)
            pool.wait_ge(v_cleared, 1)
            pool.memset(v_all[:, :, :, :, HD:HD + 1], 1.0).then_inc(v_cleared, 1)
            rstd_of(2)
            pool.memset(k_set[:], 1.0).then_inc(k_ones, 1)
            rstd_of(3)

            def keep_last(u, h):
                pool.wait_ge(qe_staged, 8 * u + 4 * h + 4)
                wait(pool, bias_fixing, 2 * (2 * (u - 1) + h + 1))
                hold(pool, pool_passed)
                pool.tensor_copy(q_last[:, h, :], qe_stage[:, h, :, NE - 1:NE].rearrange("p t o -> p (t o)")
                                 ).then_inc(q_last_ready, 1)

            def fix(u, s, h):
                head = 2 * u + h
                left = bias[:, s, h, :, 0:P]
                right = bias[:, s, h, :, 2 * P:WIN]
                pool.wait_ge(bias_loaded[h], 16 * u + 16)
                hold(pool, pool_passed)
                pool.affine_select(out=left, in_=left, compare_op=ALU.is_ge, fill=0.0, base=-1,
                                   pattern=[[0, QT], [1, P]], channel_multiplier=-1).then_inc(bias_fixing, 1)
                pool.wait_ge(q_last_ready, head + 1)
                last = q_last[:, h, :].rearrange("p (t o) -> p t o", o=1).broadcast_to([P, QT, P])
                pool.tensor_tensor(right, right, last, ALU.subtract).then_inc(bias_fixing, 1)
                pool.wait_ge(bias_fixing, 2 * head + 2)
                hold(pool, pool_passed)
                pool.affine_select(out=right, in_=right, compare_op=ALU.is_ge, fill=0.0, base=-1,
                                   pattern=[[0, QT], [-1, P]], channel_multiplier=1).then_inc(bias_ready, 1)

            def rests_of_parts():
                pool.wait_ge(v_in_psum, B)
                for i in range(2):
                    for parts, value, rest, cut, rest_made in ((q_split, q32, q_rest, q_cut_by_act, q_rest_by_pool),
                                                               (k_split, k32, k_rest, k_cut_by_act, k_rest_by_pool)):
                        dst, src = ((rest, value), (value, rest))[i]
                        pool.wait_ge(cut, i + 1)
                        pool.tensor_tensor(dst[1], src[1], parts[1][:, i, :], ALU.subtract).then_inc(rest_made, 1)

            def step(i, j, static):
                if within(static, 2, UNITS):
                    keep_last(i + 2, 1)
                    fix(i + 2, (j + 2) % SETS, 1)
                if static == -2:
                    rests_of_parts()
                if within(static, 3, UNITS):
                    keep_last(i + 3, 0)
                    fix(i + 3, (j + 3) % SETS, 0)

            for i in range(-3, 1):
                step(i, i % SETS, i)
            with pool.Fori(0, LOOPS) as turn:
                for j in range(SETS):
                    step(turn * SETS + (1 + j), (1 + j) % SETS, None)
            for i in range(1 + LOOPS * SETS, UNITS):
                step(i, i % SETS, i)

            pool.wait_ge(st_ready, 4 * QT * (UNITS - SETS + 1))
            diagonals()
            for b in range(B):
                rstd_of(4 + b)
            for b in range(B):
                x_biased_of(b, x1[:, QT * b:QT * b + QT, :])

        @block.scalar
        def _(act):
            def xn_t_copy(r):
                b = r % B
                act.wait_ge(xnt_in_psum, 2 * r + 1)
                act.copy(xn_t[b][:, 0:BANK], ps[:, bank(b, 0), :]).then_inc(xnt_by_act, 1)
                if r == 0:
                    act.wait_ge(xnt_in_psum, 2)
                    act.copy(xn_t[b][:, BANK:T], ps[:, bank(b, 1), :]).then_inc(xnt_by_act, 1)

            def s_copy(r):
                act.wait_ge(s_in_psum, r + 1)
                act.activation(s_t[:, r % B, :], ps[:, bank(r % B, 2), :], ACT.Identity, bias=bin_c).then_inc(s_by_act, 1)

            def relus(r, order=ACT_ORDER):
                act.wait_ge(s_by_act, r + 1)
                for j in order:
                    if j < PE_UNITS:
                        n = PE_UNITS * r + j
                        if n >= 4:
                            act.wait_ge(h_used, n - 3)
                        dst, done = hidden[:, n % 4, :], h_by_act
                    else:
                        if r:
                            act.wait_ge(g_step, DVE_UNITS * (r - 1) + DVE_ORDER.index(j) + 1)
                        dst, done = hidden_dve[:, j - PE_UNITS, :], h_for_dve
                    act.activation(dst, s_t[:, r % B, :], ACT.Relu, bias=b1_c[:, j:j + 1],
                                   scale=w1_c[:, j:j + 1]).then_inc(done, 1)

            def projected(b):
                for c in range(2):
                    act.wait_ge(q_in_psum, 2 * b + c + 1)
                    act.mul(q32[b][:, c * BANK:(c + 1) * BANK], ps[:, bank(b, 2 + c), :], (1.0 / HD) ** 0.5
                            ).then_inc(q_scaled, 1)
                for c in range(2):
                    act.wait_ge(k_in_psum, 2 * b + c + 1)
                    act.activation(k32[b][:, c * BANK:(c + 1) * BANK], ps[0:2 * G * HD, bank(b, c), :], ACT.Identity,
                                   bias=kshift[:, 0:1]).then_inc(k_shifted, 1)

            act.dma_start(w_row[:], w_rows).then_inc(rows_loaded, 16)
            act.dma_start(w_chan[:], w_channels).then_inc(channels_loaded, 16)
            act.dma_start(bout[:], b_out.partition_broadcast(P)).then_inc(bout_loaded, 16)
            act.dma_start(e_rev[:, 0:NE], E_t).then_inc(e_loaded, 16)
            act.dma_start(e_mask[:], e_masks).then_inc(e_loaded, 16)
            act.dma_start(kshift[:], k_shift).then_inc(e_loaded, 16)
            xn_t_copy(0)
            act.wait_ge(channels_loaded, 16)
            s_copy(0)
            relus(0)
            xn_t_copy(1)
            s_copy(1)
            relus(1, ACT_ORDER[:ACT_FIRST])
            xn_t_copy(2)
            act.wait_ge(e_loaded, 48)
            projected(0)
            relus(1, ACT_ORDER[ACT_FIRST:])

            def stage_qe(at, qe_bank):
                h, pair = key_tile(at) // 4, key_tile(at) % 4
                act.wait_ge(qe_in_psum, slot_no(at, 1, 1))
                wait(act, qe_stored[h], unit_no(at, 16))
                wait(act, q_last_ready, unit_no(at, 2, h - 1))
                act.copy(qe_stage[:, h, 2 * pair:2 * pair + 2, :].rearrange("p t w -> p (t w)"),
                         ps[:, qe_bank, :]).then_inc(qe_staged, 1)

            def slot(at, static):
                for t in range(4):
                    if within(static, 0):
                        act.wait_ge(st_ready, slot_no(at, 4, t + 1))
                        if t == 0:
                            wait(act, pv_done, slot_no(at, 1, -1))
                        act.activation(probs[:, 4 * (at[1] % 2) + t, :], ps[:, T_BANK + t % 2, :],
                                       ACT.Exp).then_inc(exp_done, 1)
                    if t == 1 and within(static, Q_LEAD) and (static is None or static + Q_LEAD >= Q_FIRST):
                        stage_qe(ahead(at, Q_LEAD), MISC)

            for n in range(QT + QT // 2):
                stage_qe((0, n), bank_of_qe(n))
            xn_t_copy(3)
            projected(1)
            for n in range(QT + QT // 2, Q_FIRST):
                stage_qe((0, n), bank_of_qe(n))
            act.wait_ge(q_scaled, 4)
            act.wait_ge(k_shifted, 4)
            for i in range(3):
                for parts, value, rest, cut, rest_made in ((q_split, q32, q_rest, q_cut_by_act, q_rest_by_pool),
                                                           (k_split, k32, k_rest, k_cut_by_act, k_rest_by_pool)):
                    if i:
                        act.wait_ge(rest_made, i)
                    act.copy(parts[1][:, i, :], (value, rest, value)[i][1]).then_inc(cut, 1)
            over_slots(act, slot)
            for b in range(B):
                act.wait_ge(at_in_psum, 2 * b + 1)
                act.copy(xn_t[b][:, 0:BANK], ps[:, bank(b, 0), :]).then_inc(at_by_act, 1)
            for r in (4, 5):
                xn_t_copy(r)
                s_copy(r - 2)
            relus(2)
            relus(3)

        @block.vector
        def _(dve):
            dve.memset(o_recip[:], 1.0).then_inc(attn_ready, 2)
            dve.memset(q_set[:], 0.0).then_inc(q_cleared, 1)

            def layer_norm(r, src):
                f, b = r // B, r % B

                def statistics(c):
                    if f == 0 and c == 0:
                        dve.wait_ge(x_loaded[b], 16)
                    if f > 0:
                        dve.wait_ge(x_new if f == 1 else x2_ready, 2 * b + c + 1)
                    for t in range(4 * c, 4 * c + 4):
                        dve.bn_stats(stats[:, QT * b + t, :], src[:, t, :]).then_inc(stats_ready, 1)

                statistics(0)
                for c in range(2):
                    if c == 0:
                        statistics(1)
                    for t in range(4 * c, 4 * c + 4):
                        dve.wait_ge(stats_ready, QT * r + t + 1)
                        dve.bn_aggr(mean_var[:, QT * b + t, :], stats[:, QT * b + t, :]).then_inc(mean_ready, 1)
                    cols = slice(QT * b + 4 * c, QT * b + 4 * c + 4)
                    dve.wait_ge(mean_ready, QT * r + 4 * c + 4)
                    dve.tensor_scalar(var_eps[:, cols], mean_var[:, cols, 1:2].rearrange("p t o -> p (t o)"), EPS, None,
                                      ALU.add).then_inc(var_ready, 1)
                for t in range(QT):
                    if t % 4 == 0:
                        dve.wait_ge(rstd_ready, 2 * r + t // 4 + 1)
                    dve.tensor_scalar(xn[b][:, t, :], src[:, t, :], mean_var[:, QT * b + t, 0:1],
                                      rstd[:, QT * b + t:QT * b + t + 1], ALU.subtract, ALU.mult).then_inc(xn_ready, 1)

            def xn_t_copy(r):
                b = r % B
                dve.wait_ge(xnt_in_psum, 2 * r + 2)
                dve.tensor_copy(xn_t[b][:, BANK:T], ps[:, bank(b, 1), :]).then_inc(xnt_by_dve, 1)

            def hidden_sum(r):
                b = r % B
                dve.wait_ge(s_by_act, r + 1)
                for i, j in enumerate(DVE_ORDER):
                    n = DVE_UNITS * r + i
                    if j >= PE_UNITS + ACT_UNITS:
                        own = OWN_UNITS * r + j - PE_UNITS - ACT_UNITS
                        if own:
                            dve.wait_ge(own_step, 2 * own)
                            dve.wait_ge(g_step, n)
                        dve.tensor_scalar(h_pre, s_t[:, b, :], w1_c[:, j:j + 1], b1_c[:, j:j + 1], ALU.mult,
                                          ALU.add).then_inc(own_step, 1)
                        dve.wait_ge(own_step, 2 * own + 1)
                        dve.tensor_scalar(hidden_own, h_pre, 0.0, None, ALU.max).then_inc(own_step, 1)
                        dve.wait_ge(own_step, 2 * own + 2)
                        unit = hidden_own
                    else:
                        dve.wait_ge(h_for_dve, ACT_UNITS * r + j - PE_UNITS + 1)
                        unit = hidden_dve[:, j - PE_UNITS, :]
                    if i == 0:
                        if r >= B:
                            dve.wait_ge(g_ready, r - 1)
                        dve.tensor_scalar(g_sum[:, b, :], unit, w2_c[:, j:j + 1], None, ALU.mult).then_inc(g_step, 1)
                    else:
                        dve.wait_ge(g_step, n)
                        dve.scalar_tensor_tensor(out=g_sum[:, b, :], in0=unit, scalar=w2_c[:, j:j + 1],
                                                 in1=g_sum[:, b, :], op0=ALU.mult, op1=ALU.add).then_inc(g_step, 1)

            def g_total(r):
                b = r % B
                dve.wait_ge(h_used, PE_UNITS * (r + 1))
                dve.wait_ge(g_step, DVE_UNITS * (r + 1))
                dve.scalar_tensor_tensor(out=g_t[:, b, :], in0=ps[:, bank(b, 3), :], scalar=b2_c, in1=g_sum[:, b, :],
                                         op0=ALU.add, op1=ALU.add).then_inc(g_ready, 1)

            def residual(r, dst):
                b = r % B
                dve.wait_ge(x_biased_ready, r + 1)
                for c in range(2):
                    dve.wait_ge(y_in_psum, 2 * r + c + 1)
                    dve.scalar_tensor_tensor(out=flat(dst[:, 4 * c:4 * c + 4, :]), in0=ps[:, bank(b, c), :], scalar=0.5,
                                             in1=flat(x_biased[b][:, 4 * c:4 * c + 4, :]),
                                             op0=ALU.mult, op1=ALU.add).then_inc(x_new, 1)

            def split(parts, value, rest, step):
                dve.tensor_copy(parts[0][:, 0, :], value[0]).then_inc(step, 1)
                dve.wait_ge(step, 1)
                dve.tensor_tensor(rest[0], value[0], parts[0][:, 0, :], ALU.subtract).then_inc(step, 1)
                dve.wait_ge(step, 2)
                dve.tensor_copy(parts[0][:, 1, :], rest[0]).then_inc(step, 1)
                dve.wait_ge(step, 3)
                dve.tensor_tensor(value[0], rest[0], parts[0][:, 1, :], ALU.subtract).then_inc(step, 1)
                dve.wait_ge(step, 4)
                dve.tensor_copy(parts[0][:, 2, :], value[0]).then_inc(step, 1)

            def place_v(b):
                dve.wait_ge(v_in_psum, b + 1)
                dve.wait_ge(v_cleared, 2)
                for t in range(QT):
                    dve.tensor_copy(v_all[:, b, :, t, 0:HD],
                                    ps[:, bank(b, 2), 32 * t:32 * t + 32].rearrange("p (g d) -> p g d", g=G)
                                    ).then_inc(v_ready, 1)

            x1_of = [x1[:, QT * b:QT * b + QT, :] for b in range(B)]
            layer_norm(0, x_in[0])
            layer_norm(1, x_in[1])
            xn_t_copy(1)
            dve.wait_ge(channels_loaded, 16)
            hidden_sum(0)
            g_total(0)
            residual(0, x1_of[0])
            layer_norm(2, x1_of[0])
            xn_t_copy(2)
            dve.wait_ge(e_loaded, 48)
            dve.tensor_copy(e_rev[:, NE:QEW], e_rev[:, NE - 1:NE]).then_inc(e_step, 1)
            dve.wait_ge(e_step, 1)
            dve.tensor_scalar(e_rel, e_rev, e_rev[:, 0:1], None, ALU.subtract).then_inc(e_step, 1)
            dve.wait_ge(e_step, 2)
            dve.tensor_copy(e_part[:, 0, :], e_rel).then_inc(e_step, 1)
            dve.wait_ge(e_step, 3)
            dve.tensor_tensor(e_rest, e_rel, e_part[:, 0, :], ALU.subtract).then_inc(e_step, 1)
            dve.wait_ge(e_step, 4)
            dve.tensor_copy(e_part[:, 1, :], e_rest).then_inc(e_step, 1)
            dve.wait_ge(e_step, 5)
            dve.tensor_tensor(e_part[:, 2, :], e_rest, e_part[:, 1, :], ALU.subtract).then_inc(e_step, 1)
            dve.wait_ge(e_step, 6)
            dve.tensor_scalar(e_rows[:], e_part[:, 0, :], e_mask[:, 0:1], None, ALU.mult).then_inc(e_ready, 1)
            for i in (1, 2):
                dve.wait_ge(e_ready, i)
                dve.scalar_tensor_tensor(out=e_rows[:], in0=e_part[:, i, :], scalar=e_mask[:, i:i + 1], in1=e_rows[:],
                                         op0=ALU.mult, op1=ALU.add).then_inc(e_ready, 1)
            dve.wait_ge(q_scaled, 2)
            split(q_split, q32, q_rest, q_split_step)
            place_v(0)
            dve.wait_ge(k_shifted, 2)
            split(k_split, k32, k_rest, k_split_step)
            hidden_sum(1)
            g_total(1)
            residual(1, x1_of[1])
            layer_norm(3, x1_of[1])
            xn_t_copy(3)
            place_v(1)

            def score_max(at, which):
                s, tile = set_of(at), 2 * key_tile(at) + which
                h, qt, par = tile // QT, tile % QT, s % 2
                near = len(near_tiles(qt)) * P
                first = (near_tiles(qt)[0] - qt + 1) * P
                base = S_BANK + 2 * which
                cols = ps[:, base:base + 2, :].rearrange("p b n -> p (b n)")
                if qt == 0:
                    dve.wait_ge(bias_ready, unit_no(at, 2, h + 1))
                dve.wait_ge(scores_ready, slot_no(at, 2, which + 1))
                wait(dve, near_done, slot_no(at, 2, which - 1))
                dve.tensor_reduce(far_max[:, par, tile:tile + 1], cols[:, near:2 * BANK], AX_X,
                                  ALU.max).then_inc(far_done, 1)
                dve.tensor_tensor_reduce(score_copy[:, tile % 2, 0:near],
                                         cols[:, 0:near],
                                         bias[:, s, h, qt, first:first + near], 1.0, -3.0e38, ALU.add, ALU.max,
                                         near_max[:, par, tile:tile + 1]).then_inc(near_done, 1)

            def unit_max(at):
                par = set_of(at) % 2
                dve.wait_ge(near_done, unit_no(at, 16, 16))
                dve.wait_ge(far_done, unit_no(at, 16, 16))
                dve.tensor_tensor(row_max[:], near_max[:, par, :], far_max[:, par, :], ALU.max).then_inc(row_max_ready, 1)

            def max_parts(at):
                dve.wait_ge(max_in_psum, unit_no(at, 1, 1))
                wait(dve, max_rows_placed, unit_no(at, 96))
                dve.tensor_scalar(neg_max[:, 0, :], ps[0:2 * QT, MISC, 0:P], -1.0, None, ALU.mult).then_inc(max_step, 1)
                dve.wait_ge(max_step, unit_no(at, 5, 1))
                dve.tensor_copy(neg_part[:, 0, :], neg_max[:, 0, :]).then_inc(max_step, 1)
                dve.wait_ge(max_step, unit_no(at, 5, 2))
                dve.tensor_tensor(neg_max[:, 1, :], neg_max[:, 0, :], neg_part[:, 0, :], ALU.subtract).then_inc(max_step, 1)
                dve.wait_ge(max_step, unit_no(at, 5, 3))
                dve.tensor_copy(neg_part[:, 1, :], neg_max[:, 1, :]).then_inc(max_step, 1)
                dve.wait_ge(max_step, unit_no(at, 5, 4))
                dve.tensor_tensor(neg_part[:, 2, :], neg_max[:, 1, :], neg_part[:, 1, :], ALU.subtract).then_inc(max_step, 1)

            def copy_out(at):
                dve.wait_ge(pv_done, unit_no(at, QT, QT))
                dve.wait_ge(attn_ready, unit_no(at, 2, 2))
                dve.tensor_copy(o_raw[:], ps[:, OUT_BANK, :]).then_inc(o_copied, 1)

            def normalise(at):
                dst = [attn[:, 4 * f:4 * f + 4, bass.ds(unit_no(at, 2 * HD), 2 * HD)]
                       .rearrange("p c (h d) -> p c h d", h=2) for f in range(2)]
                dve.wait_ge(o_in_psum, unit_no(at, 1, 1))
                o = ps[:, MISC, :].rearrange("p (c h f j) -> p c h f j", c=4, h=2, f=2)
                dve.reciprocal(o_recip[:].rearrange("p c (a o) -> p c a o", o=1),
                               ps[:, MISC, :].rearrange("p (c a j) -> p c a j", c=4, a=4)[:, :, :, HD:HD + 1]
                               ).then_inc(recip_ready, 1)
                r = o_recip[:].rearrange("p c (h f o) -> p c h f o", h=2, f=2)
                dve.wait_ge(recip_ready, unit_no(at, 1, 1))
                for f in range(2):
                    dve.tensor_tensor(dst[f], o[:, :, :, f, 0:HD], r[:, :, :, f, :].broadcast_to([P, 4, 2, HD]),
                                      ALU.mult).then_inc(attn_ready, 1)

            def slot(at, static):
                if static == -M_LEAD:
                    max_parts(ahead(at, M_LEAD))
                s_at = ahead(at, S_LEAD)
                if within(static, S_LEAD):
                    score_max(s_at, 0)
                if key_tile(at) == 0 and within(static, -QT):
                    copy_out(ahead(at, -QT))
                if key_tile(at) == QT - M_LEAD and within(static, M_LEAD) and static != -M_LEAD:
                    max_parts(ahead(at, M_LEAD))
                if key_tile(at) == 1 and within(static, -QT):
                    normalise(ahead(at, -QT))
                if within(static, S_LEAD):
                    score_max(s_at, 1)
                    if key_tile(s_at) == QT - 1:
                        unit_max(s_at)

            over_slots(dve, slot)

            for b in range(B):
                dve.wait_ge(at_in_psum, 2 * b + 2)
                dve.tensor_copy(xn_t[b][:, BANK:T], ps[:, bank(b, 1), :]).then_inc(at_by_dve, 1)
            for b in range(B):
                for c in range(2):
                    dve.wait_ge(proj_in_psum, 2 * b + c + 1)
                    cols = flat(x1_of[b][:, 4 * c:4 * c + 4, :])
                    dve.tensor_tensor(cols, ps[:, bank(b, 2 + c), :], cols, ALU.add).then_inc(x2_ready, 1)
                layer_norm(4 + b, x1_of[b])
            xn_t_copy(4)
            xn_t_copy(5)
            hidden_sum(2)
            g_total(2)
            hidden_sum(3)
            residual(2, xn[0])
            g_total(3)
            residual(3, xn[1])

        @block.tensor
        def _(pe):
            def transposes(r):
                b = r % B
                for c in range(2):
                    for t in range(4 * c, 4 * c + 4):
                        pe.wait_ge(xn_ready, QT * r + t + 1)
                        last = pe.transpose(ps[:, bank(b, c), P * (t % 4):P * (t % 4) + P], xn[b][:, t, :], ident[:])
                    last.then_inc(xnt_in_psum, 1)

            def copied(r):
                pe.wait_ge(xnt_by_act, r + 2)
                if r:
                    pe.wait_ge(xnt_by_dve, r)

            def bottleneck(r):
                b = r % B
                copied(r if r < B else r + B)
                for h in range(2):
                    last = pe.matmul(ps[M * h:M * h + M, bank(b, 2), :], win, xn_t[b][:, h * BANK:(h + 1) * BANK],
                                     start=True, stop=True)
                last.then_inc(s_in_psum, 1)

            def hidden_sum(r, units=range(PE_UNITS)):
                for j in units:
                    pe.wait_ge(diag_ready, PE_UNITS * (r // B) + j + 1)
                    pe.wait_ge(h_by_act, PE_UNITS * r + j + 1)
                    pe.matmul(ps[:, bank(r % B, 3), :], w2_diag[:, j, :], hidden[:, (PE_UNITS * r + j) % 4, :],
                              start=(j == 0), stop=(j == PE_UNITS - 1)).then_inc(h_used, 1)

            def widen(r):
                b = r % B
                pe.wait_ge(g_ready, r + 1)
                for t in range(QT):
                    rows = slice(M * (t // 4), M * (t // 4) + M)
                    last = pe.matmul(ps[:, bank(b, t // 4), P * (t % 4):P * (t % 4) + P],
                                     g_t[rows, b, P * (t % 4):P * (t % 4) + P], wout[rows, :], start=True, stop=True)
                    if t % 4 == 3:
                        last.then_inc(y_in_psum, 1)

            def project(b):
                copied(B + b)
                for c in range(2):
                    pe.matmul(ps[:, bank(b, 2 + c), :], wq, xn_t[b][:, c * BANK:(c + 1) * BANK],
                              start=True, stop=True).then_inc(q_in_psum, 1)
                for c in range(2):
                    pe.matmul(ps[0:2 * G * HD, bank(b, c), :], wk, xn_t[b][:, c * BANK:(c + 1) * BANK],
                              start=True, stop=True).then_inc(k_in_psum, 1)
                pe.wait_ge(q_scaled, 2 * b + 1)
                for t in range(QT):
                    last = pe.matmul(ps[:, bank(b, 2), 32 * t:32 * t + 32], xn_t[b][:, P * t:P * t + P], wv,
                                     start=True, stop=True)
                last.then_inc(v_in_psum, 1)

            pe.wait_ge(ident_ready, 1)
            transposes(0)
            pe.wait_ge(rows_loaded, 16)
            bottleneck(0)
            transposes(1)
            hidden_sum(0)
            bottleneck(1)
            pe.wait_ge(channels_loaded, 16)
            widen(0)
            hidden_sum(1, range(PE_FIRST))
            transposes(2)
            project(0)
            hidden_sum(1, range(PE_FIRST, PE_UNITS))

            def qe(at, qe_bank):
                s, h, pair = set_of(at), key_tile(at) // 4, key_tile(at) % 4
                if key_tile(at) == 0:
                    pe.wait_ge(q_loaded[s], loads_of(at, Q_LOADS))
                wait(pe, qe_staged, slot_no(at) if qe_bank == MISC else slot_no(at, 1, -1))
                for i in range(2):
                    qt = 2 * pair + i
                    last = pe.matmul(ps[:, qe_bank, QEW * i:QEW * i + QEW], q_set[:, s, h, P * qt:P * qt + P],
                                     e_rows[:], start=True, stop=True)
                last.then_inc(qe_in_psum, 1)

            def scores(at, which):
                s, tile = set_of(at), 2 * key_tile(at) + which
                h, qt = tile // QT, tile % QT
                near = near_tiles(qt)
                order = near + [kt for kt in range(QT) if kt not in near]
                wait(pe, near_done, slot_no(at, 2, which - 1))
                wait(pe, far_done, slot_no(at, 2, which - 1))
                i = 0
                while i < QT:
                    n = 1
                    while (i + n < QT and order[i + n] == order[i] + n and (i + n) % 4
                           and (order[i + n] > qt) == (order[i] > qt)):
                        n += 1
                    kt = order[i]
                    last = pe.matmul(ps[:, S_BANK + 2 * which + i // 4, P * (i % 4):P * (i % 4 + n)],
                                     q_set[:, s, h, P * qt:P * qt + P],
                                     k_set[:, s, int(kt > qt), P * kt:P * (kt + n)], start=True, stop=True)
                    i += n
                last.then_inc(scores_ready, 1)

            def exponents(at, t):
                s, kt = set_of(at), key_tile(at)
                h, half = t // 2, t % 2
                bank = T_BANK + t % 2
                wait(pe, exp_done, slot_no(at, 4, t - 1))
                first = True
                for i in range(4):
                    qt = 4 * half + i
                    if abs(qt - kt) <= 1:
                        w = (kt - qt + 1) * P
                        pe.matmul(ps[:, bank, P * i:P * i + P], bias[:, s, h, qt, w:w + P], ident[:],
                                  is_transpose=True, start=first, stop=False, skip_group_check=True)
                        first = False
                cut = min(max(kt - 4 * half, 0), 4)
                for var, a, b in ((1, 0, cut), (0, cut, 4)):
                    if a < b:
                        last = pe.matmul(ps[:, bank, P * a:P * b], k_set[:, s, var, P * kt:P * kt + P],
                                         q_set[:, s, h, P * (4 * half + a):P * (4 * half + b)],
                                         start=first, stop=True, skip_group_check=True)
                        first = False
                last.then_inc(st_ready, 1)

            def weigh(at):
                s, kt = set_of(at), key_tile(at)
                if kt == 0:
                    wait(pe, o_copied, unit_no(at))
                pe.wait_ge(exp_done, slot_no(at, 4, 4))
                for t in range(4):
                    last = pe.matmul(ps[32 * t:32 * t + 32, OUT_BANK, :], v_set[:, s, kt, :],
                                     probs[:, 4 * (at[1] % 2) + t, :], start=(kt == 0), stop=(kt == QT - 1))
                last.then_inc(pv_done, 1)

            def max_to_rows(at):
                pe.wait_ge(row_max_ready, unit_no(at, 1, 1))
                pe.transpose(ps[0:2 * QT, MISC, 0:P], row_max[:], ident[:]).then_inc(max_in_psum, 1)

            def outputs_to_rows(at):
                pe.wait_ge(o_copied, unit_no(at, 1, 1))
                for c in range(4):
                    last = pe.transpose(ps[:, MISC, P * c:P * c + P], o_raw[:, P * c:P * c + P], ident[:])
                last.then_inc(o_in_psum, 1)

            def misc_free(at, static, of_slot):
                if of_slot and within(static, Q_LEAD):
                    pe.wait_ge(qe_staged, slot_no(at, 1, Q_LEAD + 1))
                elif within(static, Q_LEAD - 1):
                    pe.wait_ge(qe_staged, slot_no(at, 1, Q_LEAD))

            def slot(at, static):
                kt = key_tile(at)
                s_at = ahead(at, S_LEAD)
                if within(static, 0):
                    if kt == 0:
                        pe.wait_ge(max_rows_placed, unit_no(at, 96, 96))
                        pe.wait_ge(bias_ready, unit_no(at, 2, 2))
                    exponents(at, 0)
                if static == -M_LEAD:
                    misc_free(at, static, False)
                    max_to_rows(ahead(at, M_LEAD))
                if within(static, S_LEAD):
                    if key_tile(s_at) == 0:
                        pe.wait_ge(kv_loaded[set_of(s_at)], loads_of(s_at, KV_LOADS))
                    scores(s_at, 0)
                if within(static, 0):
                    exponents(at, 1)
                if within(static, Q_LEAD) and (static is None or static + Q_LEAD >= Q_FIRST):
                    if (kt == QT - M_LEAD + 1 and within(static, M_LEAD)) or static == -M_LEAD:
                        pe.wait_ge(max_step, unit_no(ahead(at, M_LEAD), 5, 1))
                    if kt == 2 and within(static, -QT):
                        pe.wait_ge(attn_ready, unit_no(ahead(at, -QT), 2, 4))
                    qe(ahead(at, Q_LEAD), MISC)
                if static in (-S_LEAD, 1 - S_LEAD):
                    for n in range(2):
                        n += Q_FIRST - 4 + 2 * (static + S_LEAD)
                        qe((0, n), bank_of_qe(n))
                if within(static, 0):
                    exponents(at, 2)
                if within(static, -1):
                    weigh(ahead(at, -1))
                if kt == QT - M_LEAD and within(static, M_LEAD) and static != -M_LEAD:
                    misc_free(at, static, True)
                    max_to_rows(ahead(at, M_LEAD))
                if kt == 1 and within(static, -QT):
                    misc_free(at, static, True)
                    outputs_to_rows(ahead(at, -QT))
                if within(static, 0):
                    exponents(at, 3)
                if within(static, S_LEAD):
                    scores(s_at, 1)

            pe.wait_ge(q_scaled, 2)
            pe.wait_ge(k_shifted, 2)
            pe.wait_ge(e_ready, 3)
            for n in range(QT):
                qe((0, n), bank_of_qe(n))
            widen(1)
            for n in range(QT, QT + QT // 2):
                qe((0, n), bank_of_qe(n))
            transposes(3)
            project(1)
            pe.wait_ge(q_scaled, 4)
            pe.wait_ge(k_shifted, 4)
            pe.wait_ge(v_ready, NT)
            over_slots(pe, slot)

            pe.wait_ge(attn_ready, 2 * UNITS + 2)
            for b in range(B):
                for qt in range(QT):
                    last = pe.transpose(ps[:, bank(b, qt // 4), P * (qt % 4):P * (qt % 4) + P],
                                        attn[:, qt, b * D:b * D + D], ident[:])
                    if qt % 4 == 3:
                        last.then_inc(at_in_psum, 1)
            for b in range(B):
                pe.wait_ge(at_by_act, b + 1)
                pe.wait_ge(at_by_dve, b + 1)
                for t in range(QT):
                    last = pe.matmul(ps[:, bank(b, 2 + t // 4), P * (t % 4):P * (t % 4) + P],
                                     xn_t[b][:, P * t:P * t + P], wo, start=True, stop=True)
                    if t % 4 == 3:
                        last.then_inc(proj_in_psum, 1)
            for b in range(B):
                transposes(4 + b)
                bottleneck(2 + b)
            hidden_sum(2)
            widen(2)
            hidden_sum(3)
            widen(3)


def kernel(L0_attn_x, L0_attn_Wq, L0_attn_Wk, L0_attn_Wv, L0_attn_Wo, L0_attn_E, L0_ffn_Win, L0_ffn_bin_,
           L0_ffn_W1, L0_ffn_b1, L0_ffn_W2, L0_ffn_b2, L0_ffn_Wout, L0_ffn_bout):
    import numpy as np
    import concourse.bacc as bacc
    from concourse import mybir as my
    from concourse.bass_utils import run_bass_kernel_spmd

    E = np.asarray(L0_attn_E)
    win, wq, wk, wv, wo = (np.asarray(L0_ffn_Win), np.asarray(L0_attn_Wq).T, np.asarray(L0_attn_Wk).T,
                           np.asarray(L0_attn_Wv).T, np.asarray(L0_attn_Wo).T)
    channels = np.concatenate([np.asarray(L0_ffn_bin_)[:, None], L0_ffn_W1, L0_ffn_b1, L0_ffn_W2,
                               np.asarray(L0_ffn_b2)[:, None], L0_ffn_Wout], axis=1)
    masks = np.zeros((P, 3), np.float32)
    for base in (0, HB):
        for r, k in enumerate(K_PART):
            masks[base + HD * r:base + HD * r + HD, k] = 1.0
    arrays = {
        "x": np.asarray(L0_attn_x).reshape(B * T, D),
        "w_rows": np.concatenate([win, wq, wk, wk, wv, wo], axis=1),
        "w_channels": np.concatenate([channels, channels], axis=0),
        "E_t": np.tile(E[::-1].T, (P // HD, 1)),
        "e_masks": masks,
        "k_shift": np.concatenate([np.tile(E[NE - 1], G), np.tile(E[0], G)])[:, None],
        "b_out": L0_ffn_bout,
    }
    nc = bacc.Bacc("TRN2", target_bir_lowering=False, num_devices=1)
    feeds, args = {}, []
    for name, a in arrays.items():
        a = np.ascontiguousarray(a)
        feeds[f"in_{name}"] = a
        args.append(nc.dram_tensor(f"in_{name}", a.shape, my.dt.from_np(a.dtype), kind="ExternalInput").ap())
    args.append(nc.dram_tensor("out", [B * T, D], F32, kind="ExternalOutput").ap())
    macaron_attention(nc, *args)
    r = run_bass_kernel_spmd(nc, [feeds], core_ids=[0])
    return r.results[0]["out"].reshape(B, T, D)
```
